# Optimizing a Trainium2 kernel written in Bass

```python
import numpy as np
import jax
import jax.numpy as jnp

def _softmax(x, axis=-1):
    return jax.nn.softmax(x, axis=axis)

def _gelu(x):
    return jax.nn.gelu(x, approximate=True)

def _silu(x):
    return jax.nn.silu(x)

def _sigmoid(x):
    return jax.nn.sigmoid(x)

def _layernorm(x, axis=-1, eps=1e-05):
    m = jnp.mean(x, axis=axis, keepdims=True)
    v = jnp.var(x, axis=axis, keepdims=True)
    return (x - m) / jnp.sqrt(v + eps)

def _scatter_add(tgt, idx, src, axis=0):
    return tgt.at[idx].add(src)

def _segment_sum(src, seg, n):
    return jax.ops.segment_sum(src, seg, n)
kernel_name = 'mk_recurrent_d2_jaxref_r8_3583fe'

def setup_inputs(seed: int=0):
    np.random.seed(seed)
    _w = jnp.asarray

    def _L0_attn_setup():
        import jax, jax.numpy as jnp
        import numpy as np
        H, HD, D = (16, 64, 128)
        SCALE = HD ** (-0.5)
        TEMP = 1.0
        EPS = 1e-05
        key = jax.random.key(seed)
        ks = jax.random.split(key, 10)
        B, N = (2, 256)
        lim = 1.0 / np.sqrt(D)

        def lin(k, out_d, in_d):
            k1, k2 = jax.random.split(k)
            W = jax.random.uniform(k1, (out_d, in_d), jnp.float32, -lim, lim)
            b = jax.random.uniform(k2, (out_d,), jnp.float32, -lim, lim)
            return (W, b)
        Wq, bq = lin(ks[0], H * HD, D)
        Wk, bk = lin(ks[1], H * HD, D)
        Wv, bv = lin(ks[2], H * HD, D)
        Wo, bo = lin(ks[3], D, H * HD)
        return {'x': jax.random.normal(ks[4], (B, N, D), jnp.float32), 'adaptive_scale': jnp.ones((H,), jnp.float32), 'Wq': Wq, 'bq': bq, 'Wk': Wk, 'bk': bk, 'Wv': Wv, 'bv': bv, 'Wo': Wo, 'bo': bo, 'gamma': jnp.ones((D,), jnp.float32), 'beta': jnp.zeros((D,), jnp.float32)}
    _L0_attn_in = _L0_attn_setup()

    def _L0_ffn_setup():
        import jax, jax.numpy as jnp
        import numpy as np
        S, B, D, H, E, K, F = (128, 4, 128, 16, 8, 2, 512)

        def _ln(x, g, b, eps=1e-05):
            mu = jnp.mean(x, axis=-1, keepdims=True)
            var = jnp.mean((x - mu) ** 2, axis=-1, keepdims=True)
            return (x - mu) * jax.lax.rsqrt(var + eps) * g + b
        key = jax.random.key(seed)
        ks = jax.random.split(key, 8)
        s = 0.02
        return {'src': jax.random.normal(ks[0], (S, B, D), jnp.float32), 'in_proj_w': jax.random.normal(ks[1], (3 * D, D), jnp.float32) * s, 'in_proj_b': jnp.zeros((3 * D,), jnp.float32), 'out_w': jax.random.normal(ks[2], (D, D), jnp.float32) * s, 'out_b': jnp.zeros((D,), jnp.float32), 'gate_w': jax.random.normal(ks[3], (E, D), jnp.float32) * s, 'gate_b': jnp.zeros((E,), jnp.float32), 'w1': jax.random.normal(ks[4], (E, F, D), jnp.float32) * s, 'b1': jnp.zeros((E, F), jnp.float32), 'w2': jax.random.normal(ks[5], (E, D, F), jnp.float32) * s, 'b2': jnp.zeros((E, D), jnp.float32), 'ln1_g': jnp.ones((D,), jnp.float32), 'ln1_b': jnp.zeros((D,), jnp.float32), 'ln2_g': jnp.ones((D,), jnp.float32), 'ln2_b': jnp.zeros((D,), jnp.float32)}
    _L0_ffn_in = _L0_ffn_setup()

    def _L1_attn_setup():
        import jax, jax.numpy as jnp
        import numpy as np
        B, T, IN_DIM, EMB = (8, 256, 128, 128)
        NEG_INF = -1e+30
        key = jax.random.key(seed)
        ks = jax.random.split(key, 7)
        s = 1.0 / np.sqrt(IN_DIM)
        return {'x': jax.random.normal(ks[0], (B, T, IN_DIM), dtype=jnp.float32), 'Wq': jax.random.normal(ks[1], (IN_DIM, EMB), dtype=jnp.float32) * s, 'bq': jax.random.normal(ks[2], (EMB,), dtype=jnp.float32) * 0.01, 'Wk': jax.random.normal(ks[3], (IN_DIM, EMB), dtype=jnp.float32) * s, 'bk': jax.random.normal(ks[4], (EMB,), dtype=jnp.float32) * 0.01, 'Wv': jax.random.normal(ks[5], (IN_DIM, EMB), dtype=jnp.float32) * s, 'bv': jax.random.normal(ks[6], (EMB,), dtype=jnp.float32) * 0.01}
    _L1_attn_in = _L1_attn_setup()

    def _L1_ffn_setup():
        import jax, jax.numpy as jnp
        import numpy as np
        D_MODEL = 128
        HIDDEN = 256
        N_EXPERTS = 8
        TOP_K = 2
        BATCH = 2
        SEQ = 256
        key = jax.random.key(seed)
        ks = jax.random.split(key, 9)
        s = 0.02
        return {'x': jax.random.normal(ks[0], (BATCH, SEQ, D_MODEL), dtype=jnp.float32), 'w_router': jax.random.normal(ks[1], (D_MODEL, N_EXPERTS), dtype=jnp.float32) * s, 'w1': jax.random.normal(ks[2], (N_EXPERTS, D_MODEL, HIDDEN), dtype=jnp.float32) * s, 'w3': jax.random.normal(ks[3], (N_EXPERTS, D_MODEL, HIDDEN), dtype=jnp.float32) * s, 'w2': jax.random.normal(ks[4], (N_EXPERTS, HIDDEN, D_MODEL), dtype=jnp.float32) * s, 'sw1': jax.random.normal(ks[5], (D_MODEL, HIDDEN), dtype=jnp.float32) * s, 'sw3': jax.random.normal(ks[6], (D_MODEL, HIDDEN), dtype=jnp.float32) * s, 'sw2': jax.random.normal(ks[7], (HIDDEN, D_MODEL), dtype=jnp.float32) * s}
    _L1_ffn_in = _L1_ffn_setup()
    _d = {'L0_attn_x': _L0_attn_in['x'], 'L0_attn_adaptive_scale': _L0_attn_in['adaptive_scale'], 'L0_attn_Wq': _L0_attn_in['Wq'], 'L0_attn_bq': _L0_attn_in['bq'], 'L0_attn_Wk': _L0_attn_in['Wk'], 'L0_attn_bk': _L0_attn_in['bk'], 'L0_attn_Wv': _L0_attn_in['Wv'], 'L0_attn_bv': _L0_attn_in['bv'], 'L0_attn_Wo': _L0_attn_in['Wo'], 'L0_attn_bo': _L0_attn_in['bo'], 'L0_attn_gamma': _L0_attn_in['gamma'], 'L0_attn_beta': _L0_attn_in['beta'], 'L0_ffn_in_proj_w': _L0_ffn_in['in_proj_w'], 'L0_ffn_in_proj_b': _L0_ffn_in['in_proj_b'], 'L0_ffn_out_w': _L0_ffn_in['out_w'], 'L0_ffn_out_b': _L0_ffn_in['out_b'], 'L0_ffn_gate_w': _L0_ffn_in['gate_w'], 'L0_ffn_gate_b': _L0_ffn_in['gate_b'], 'L0_ffn_w1': _L0_ffn_in['w1'], 'L0_ffn_b1': _L0_ffn_in['b1'], 'L0_ffn_w2': _L0_ffn_in['w2'], 'L0_ffn_b2': _L0_ffn_in['b2'], 'L0_ffn_ln1_g': _L0_ffn_in['ln1_g'], 'L0_ffn_ln1_b': _L0_ffn_in['ln1_b'], 'L0_ffn_ln2_g': _L0_ffn_in['ln2_g'], 'L0_ffn_ln2_b': _L0_ffn_in['ln2_b'], 'L1_attn_Wq': _L1_attn_in['Wq'], 'L1_attn_bq': _L1_attn_in['bq'], 'L1_attn_Wk': _L1_attn_in['Wk'], 'L1_attn_bk': _L1_attn_in['bk'], 'L1_attn_Wv': _L1_attn_in['Wv'], 'L1_attn_bv': _L1_attn_in['bv'], 'L1_ffn_w_router': _L1_ffn_in['w_router'], 'L1_ffn_w1': _L1_ffn_in['w1'], 'L1_ffn_w3': _L1_ffn_in['w3'], 'L1_ffn_w2': _L1_ffn_in['w2'], 'L1_ffn_sw1': _L1_ffn_in['sw1'], 'L1_ffn_sw3': _L1_ffn_in['sw3'], 'L1_ffn_sw2': _L1_ffn_in['sw2']}
    _x0 = _d['L0_attn_x']
    _d['L0_attn_x'] = jax.random.normal(jax.random.fold_in(jax.random.key(seed), 1), (1, 2048, 128), dtype=_x0.dtype)
    del _x0
    return _d

def reference(L0_attn_x, L0_attn_adaptive_scale, L0_attn_Wq, L0_attn_bq, L0_attn_Wk, L0_attn_bk, L0_attn_Wv, L0_attn_bv, L0_attn_Wo, L0_attn_bo, L0_attn_gamma, L0_attn_beta, L0_ffn_in_proj_w, L0_ffn_in_proj_b, L0_ffn_out_w, L0_ffn_out_b, L0_ffn_gate_w, L0_ffn_gate_b, L0_ffn_w1, L0_ffn_b1, L0_ffn_w2, L0_ffn_b2, L0_ffn_ln1_g, L0_ffn_ln1_b, L0_ffn_ln2_g, L0_ffn_ln2_b, L1_attn_Wq, L1_attn_bq, L1_attn_Wk, L1_attn_bk, L1_attn_Wv, L1_attn_bv, L1_ffn_w_router, L1_ffn_w1, L1_ffn_w3, L1_ffn_w2, L1_ffn_sw1, L1_ffn_sw3, L1_ffn_sw2):

    def _L0_attn_ref(x, adaptive_scale, Wq, bq, Wk, bk, Wv, bv, Wo, bo, gamma, beta):
        import jax, jax.numpy as jnp
        import numpy as np
        H, HD, D = (16, 64, 128)
        SCALE = HD ** (-0.5)
        TEMP = 1.0
        EPS = 1e-05
        B, N, _ = x.shape
        Q = (x @ Wq.T + bq).reshape(B, N, H, HD)
        K = (x @ Wk.T + bk).reshape(B, N, H, HD)
        V = (x @ Wv.T + bv).reshape(B, N, H, HD)
        scores = jnp.einsum('bnhd,bmhd->bhnm', Q, K)
        scores = scores * (SCALE * adaptive_scale)[None, :, None, None] / TEMP
        w = jax.nn.softmax(scores, axis=-1)
        attn = jnp.einsum('bhnm,bmhd->bnhd', w, V).reshape(B, N, H * HD)
        y = x + (attn @ Wo.T + bo)
        mu = jnp.mean(y, axis=-1, keepdims=True)
        var = jnp.var(y, axis=-1, keepdims=True)
        return (y - mu) / jnp.sqrt(var + EPS) * gamma + beta

    def _L0_ffn_ref(src, in_proj_w, in_proj_b, out_w, out_b, gate_w, gate_b, w1, b1, w2, b2, ln1_g, ln1_b, ln2_g, ln2_b):
        import jax, jax.numpy as jnp
        import numpy as np
        S, B, D, H, E, K, F = (128, 4, 128, 16, 8, 2, 512)

        def _ln(x, g, b, eps=1e-05):
            mu = jnp.mean(x, axis=-1, keepdims=True)
            var = jnp.mean((x - mu) ** 2, axis=-1, keepdims=True)
            return (x - mu) * jax.lax.rsqrt(var + eps) * g + b
        s_len, bsz, d = src.shape
        dh = d // H
        qkv = src @ in_proj_w.T + in_proj_b
        q, k, v = jnp.split(qkv, 3, axis=-1)
        q = q.reshape(s_len, bsz, H, dh)
        k = k.reshape(s_len, bsz, H, dh)
        v = v.reshape(s_len, bsz, H, dh)
        scale = dh ** (-0.5)
        scores = jnp.einsum('sbhd,tbhd->bhst', q, k) * scale
        attn = jax.nn.softmax(scores, axis=-1)
        ctx = jnp.einsum('bhst,tbhd->sbhd', attn, v).reshape(s_len, bsz, d)
        attn_out = ctx @ out_w.T + out_b
        x = _ln(src + attn_out, ln1_g, ln1_b)
        tok = x.reshape(-1, d)
        n_tok = tok.shape[0]
        logits = tok @ gate_w.T + gate_b
        probs = jax.nn.softmax(logits, axis=-1)
        topv, topi = jax.lax.top_k(probs, K)
        topv = topv / jnp.sum(topv, axis=-1, keepdims=True)
        combine = jnp.zeros_like(probs).at[jnp.arange(n_tok)[:, None], topi].set(topv)
        moe_out = jnp.zeros_like(tok)
        for e in range(E):
            h = jax.nn.relu(tok @ w1[e].T + b1[e]) @ w2[e].T + b2[e]
            moe_out = moe_out + combine[:, e:e + 1] * h
        moe_out = moe_out.reshape(s_len, bsz, d)
        return _ln(x + moe_out, ln2_g, ln2_b)

    def _L1_attn_ref(x, Wq, bq, Wk, bk, Wv, bv):
        import jax, jax.numpy as jnp
        import numpy as np
        B, T, IN_DIM, EMB = (8, 256, 128, 128)
        NEG_INF = -1e+30
        q = x @ Wq + bq
        k = x @ Wk + bk
        v = x @ Wv + bv
        scale = jnp.asarray(EMB, x.dtype) ** 0.5
        scores = jnp.einsum('btd,bsd->bts', q, k) / scale
        Tq = scores.shape[-2]
        causal = jnp.tril(jnp.ones((Tq, Tq), dtype=bool))
        scores = jnp.where(causal, scores, jnp.asarray(NEG_INF, scores.dtype))
        m = jnp.max(scores, axis=(-2, -1), keepdims=True)
        e = jnp.exp(scores - m)
        w = e / jnp.sum(e, axis=(-2, -1), keepdims=True)
        return jnp.einsum('bts,bsd->btd', w, v)

    def _L1_ffn_ref(x, w_router, w1, w3, w2, sw1, sw3, sw2):
        import jax, jax.numpy as jnp
        import numpy as np
        D_MODEL = 128
        HIDDEN = 256
        N_EXPERTS = 8
        TOP_K = 2
        BATCH = 2
        SEQ = 256
        b, s, d = x.shape
        xf = x.reshape(b * s, d)
        probs = jax.nn.softmax(xf @ w_router, axis=-1)
        top_vals, top_idx = jax.lax.top_k(probs, TOP_K)
        gates = top_vals / jnp.sum(top_vals, axis=-1, keepdims=True)
        onehot = jax.nn.one_hot(top_idx, N_EXPERTS, dtype=xf.dtype)
        cw = jnp.einsum('tk,tke->te', gates, onehot)
        h1 = jnp.einsum('td,edh->eth', xf, w1)
        h3 = jnp.einsum('td,edh->eth', xf, w3)
        y = jnp.einsum('eth,ehd->etd', jax.nn.silu(h1) * h3, w2)
        out = jnp.einsum('etd,te->td', y, cw)
        out = out + jax.nn.silu(xf @ sw1) * (xf @ sw3) @ sw2
        return out.reshape(b, s, d)
    x = L0_attn_x
    xn = _layernorm(x, axis=-1)
    s = _L0_attn_ref(xn, L0_attn_adaptive_scale, L0_attn_Wq, L0_attn_bq, L0_attn_Wk, L0_attn_bk, L0_attn_Wv, L0_attn_bv, L0_attn_Wo, L0_attn_bo, L0_attn_gamma, L0_attn_beta)
    g = _silu(_L0_ffn_ref(xn, L0_ffn_in_proj_w, L0_ffn_in_proj_b, L0_ffn_out_w, L0_ffn_out_b, L0_ffn_gate_w, L0_ffn_gate_b, L0_ffn_w1, L0_ffn_b1, L0_ffn_w2, L0_ffn_b2, L0_ffn_ln1_g, L0_ffn_ln1_b, L0_ffn_ln2_g, L0_ffn_ln2_b))
    x = x + s * g
    xn = _layernorm(x, axis=-1)
    s = _L1_attn_ref(xn, L1_attn_Wq, L1_attn_bq, L1_attn_Wk, L1_attn_bk, L1_attn_Wv, L1_attn_bv)
    g = _silu(_L1_ffn_ref(xn, L1_ffn_w_router, L1_ffn_w1, L1_ffn_w3, L1_ffn_w2, L1_ffn_sw1, L1_ffn_sw3, L1_ffn_sw2))
    x = x + s * g
    return x

_drawn_inputs = setup_inputs


def setup_inputs(seed=0):
    import zlib

    import numpy as np

    out = dict(_drawn_inputs(seed))
    spreads = {'L0_attn_adaptive_scale': (1.0, 0.6),
     'L0_attn_gamma': (1.0, 0.2),
     'L0_attn_beta': (0.0, 0.282),
     'L0_ffn_in_proj_b': (0.0, 0.711),
     'L0_ffn_out_b': (0.0, 0.1),
     'L0_ffn_gate_b': (0.0, 0.331),
     'L0_ffn_b1': (0.0, 0.8),
     'L0_ffn_b2': (0.0, 0.323),
     'L0_ffn_ln1_g': (1.0, 0.2),
     'L0_ffn_ln1_b': (0.0, 0.1),
     'L0_ffn_ln2_g': (1.0, 0.2),
     'L0_ffn_ln2_b': (0.0, 0.1)}
    factors = {'L0_attn_Wq': 4.971,
     'L0_attn_bq': 8.0,
     'L0_attn_Wk': 4.843,
     'L0_attn_bk': 200.0,
     'L0_attn_Wv': 4.209,
     'L0_attn_bo': 3.087,
     'L0_ffn_w1': 3.232,
     'L1_attn_Wq': 8.0,
     'L1_attn_bq': 64.0,
     'L1_attn_Wk': 8.0,
     'L1_attn_bk': 200.0,
     'L1_attn_Wv': 8.0,
     'L1_attn_bv': 57.539,
     'L1_ffn_w_router': 8.0,
     'L1_ffn_w1': 8.0,
     'L1_ffn_w3': 8.0,
     'L1_ffn_w2': 8.0,
     'L1_ffn_sw1': 8.0,
     'L1_ffn_sw3': 8.0,
     'L1_ffn_sw2': 8.0,
     'L0_attn_bv': 3.542}
    for name, (base, spread) in spreads.items():
        noise = np.random.default_rng([zlib.crc32(name.encode()), seed]).standard_normal(out[name].shape)
        drawn = base * np.exp(spread * noise) if base else spread * noise
        out[name] = jnp.asarray(drawn.astype(out[name].dtype))
    for name, factor in factors.items():
        out[name] = (out[name] * factor).astype(out[name].dtype)
    return out
```

```python
from contextlib import ExitStack

import concourse.bass as bass
from concourse import mybir

F32 = mybir.dt.float32
F32R = mybir.dt.float32r
BF16 = mybir.dt.bfloat16
F16 = mybir.dt.float16
ALU = mybir.AluOpType
ACT = mybir.ActivationFunctionType
AX_X = mybir.AxisListType.X

P = 128
N = 2048
D = 128
NT = N // P
BLK = 512
NB = N // BLK
TPB = BLK // P
H = 16
HD = 64
VW = 2 * HD + 1
E0 = 8
FT0 = 4
E1 = 9
FT1 = 2
EPS = 1e-5
BIG = 1e30

C_BO, C_VB, C_OUTB, C_Q1B, C_K1B = range(5)
C_B1 = 5
NCOL = C_B1 + E0 * FT0
ROWS = {}
_at = 0
for _n, _w in (("ln1_g", D), ("ln1_b", D), ("ln2_g", D), ("ln2_b", D), ("gamma", D), ("beta", D),
               ("v1b", D), ("gate_b", E0)):
    ROWS[_n] = (_at, _w)
    _at += _w
NROW = _at


class Count:

    def __init__(self, i, times, plus):
        self.i, self.times, self.plus = i, times, plus

    def __add__(self, c):
        return Count(self.i, self.times, self.plus + c)

    def __sub__(self, c):
        return self + -c

    def __mul__(self, c):
        return Count(self.i, self.times * c, self.plus * c)

    def value(self):
        return self.i * self.times + self.plus


BASES = {}


def ge(eng, sem, value):
    if isinstance(value, Count):
        if not isinstance(value.i, int):
            key = (id(value.i), sem.name, value.times)
            if key not in BASES:
                register = eng.alloc_register(f"{sem.name}_base")
                eng.reg_mul(register, value.i, value.times)
                BASES[key] = eng.snap(register, donate=True)
            value = BASES[key] + value.plus
        else:
            value = value.value()
    if not (isinstance(value, int) and value <= 0):
        eng.wait_ge(sem, value)


def spread(ap, n):
    return ap.rearrange("p (o w) -> p o w", o=1).broadcast_to([P, n, ap.shape[1]])


def each(ap, w):
    return ap.rearrange("p (n o) -> p n o", o=1).broadcast_to([P, ap.shape[1], w])


class Norm:

    def __init__(self, ctx, nc, name):
        self.bn = ctx.enter_context(nc.semaphore(f"{name}_bn"))
        self.mv = ctx.enter_context(nc.semaphore(f"{name}_mv"))
        self.var = ctx.enter_context(nc.semaphore(f"{name}_var"))
        self.sd = ctx.enter_context(nc.semaphore(f"{name}_sd"))
        self.r = ctx.enter_context(nc.semaphore(f"{name}_rstd"))
        sb = lambda what, w: ctx.enter_context(nc.sbuf_tensor(f"{name}_{what}", [P, w], F32))
        self.st = sb("stats", NT * 6)
        self.mean_var = sb("mean_var", NT * 2)
        self.ve, self.root, self.rstd, self.t = (sb(w, NT) for w in ("ve", "root", "rstd", "t"))

    def mean(self, t):
        return self.mean_var[:, 2 * t:2 * t + 1]

    def vector(self, dve, src, ready=None):
        for t in range(NT):
            if ready:
                ready(t)
            dve.bn_stats(self.st[:, 6 * t:6 * t + 6], src[:, t * D:(t + 1) * D]).then_inc(self.bn, 1)
        for t in range(NT):
            dve.wait_ge(self.bn, t + 1)
            dve.bn_aggr(self.mean_var[:, 2 * t:2 * t + 2], self.st[:, 6 * t:6 * t + 6]).then_inc(self.mv, 1)
        dve.wait_ge(self.mv, NT)
        var = self.mean_var[:, :].rearrange("p (t c) -> p t c", c=2)[:, :, 1]
        dve.tensor_scalar(self.ve[:, :], var, EPS, None, ALU.add).then_inc(self.var, 1)
        dve.wait_ge(self.sd, 1)
        dve.reciprocal(self.rstd[:, :], self.root[:, :]).then_inc(self.r, 1)
        dve.wait_ge(self.r, 1)
        dve.tensor_tensor(self.t[:, :], self.rstd[:, :], self.rstd[:, :], ALU.mult).then_inc(self.r, 1)
        dve.wait_ge(self.r, 2)
        dve.tensor_tensor(self.t[:, :], self.t[:, :], self.ve[:, :], ALU.mult).then_inc(self.r, 1)
        dve.wait_ge(self.r, 3)
        dve.tensor_scalar(self.t[:, :], self.t[:, :], -0.5, 1.5, ALU.mult, ALU.add).then_inc(self.r, 1)
        dve.wait_ge(self.r, 4)
        dve.tensor_tensor(self.rstd[:, :], self.rstd[:, :], self.t[:, :], ALU.mult).then_inc(self.r, 1)
        dve.wait_ge(self.r, 5)

    def scalar(self, act):
        act.wait_ge(self.var, 1)
        act.activation(self.root[:, :], self.ve[:, :], ACT.Sqrt).then_inc(self.sd, 1)

    def apply(self, dve, dst, src, t, done):
        dve.tensor_scalar(dst[:, t * D:(t + 1) * D], src[:, t * D:(t + 1) * D], self.mean(t),
                          self.rstd[:, t:t + 1], ALU.subtract, ALU.mult).then_inc(done, 1)


class Router:

    def __init__(self, ctx, nc, name):
        self.sem = ctx.enter_context(nc.semaphore(f"{name}_route"))
        self.ex = ctx.enter_context(nc.semaphore(f"{name}_route_exp"))
        sb = lambda what, w: ctx.enter_context(nc.sbuf_tensor(f"{name}_{what}", [P, w], F32))
        self.lg, self.pr, self.eq, self.one, self.rest, self.two, self.w = (
            sb(x, NT * E0) for x in ("logits", "probs", "eq", "first", "rest", "second", "combine"))
        self.m = sb("top", NT)
        self.order = ctx.enter_context(nc.sbuf_tensor(f"{name}_order", [P, NT * E0], F32))
        self.n = 0

    def v(self, t):
        return t[:, :].rearrange("p (t e) -> p t e", e=E0)

    def step(self, dve, ins):
        self.n += 1
        ins.then_inc(self.sem, 1)
        dve.wait_ge(self.sem, self.n)

    def vector(self, dve, logits_psum, bias):
        v, m = self.v, self.m
        for e in range(E0):
            self.step(dve, dve.memset(v(self.order)[:, :, e], float(E0 - e)))
        if bias is None:
            self.step(dve, dve.tensor_copy(self.lg[:, :], logits_psum))
        else:
            self.step(dve, dve.tensor_tensor(v(self.lg), logits_psum.rearrange("p (t e) -> p t e", e=E0),
                                             spread(bias, NT), ALU.add))
        self.step(dve, dve.tensor_reduce(m[:, :], v(self.lg), AX_X, ALU.max))
        self.step(dve, dve.tensor_tensor(v(self.lg), v(self.lg), each(m[:, :], E0), ALU.subtract))
        dve.wait_ge(self.ex, 1)
        self.step(dve, dve.tensor_reduce(m[:, :], v(self.pr), AX_X, ALU.add))
        self.step(dve, dve.reciprocal(m[:, :], m[:, :]))
        self.step(dve, dve.tensor_tensor(v(self.pr), v(self.pr), each(m[:, :], E0), ALU.mult))
        self.pick(dve, self.pr, self.one)
        self.step(dve, dve.tensor_tensor(self.rest[:, :], self.pr[:, :], self.one[:, :], ALU.subtract))
        self.step(dve, dve.tensor_tensor(self.rest[:, :], self.rest[:, :], self.one[:, :], ALU.subtract))
        self.pick(dve, self.rest, self.two)
        self.step(dve, dve.tensor_tensor(self.one[:, :], self.one[:, :], self.two[:, :], ALU.add))
        self.step(dve, dve.tensor_tensor(self.w[:, :], self.pr[:, :], self.one[:, :], ALU.mult))
        self.step(dve, dve.tensor_reduce(m[:, :], v(self.w), AX_X, ALU.add))
        self.step(dve, dve.reciprocal(m[:, :], m[:, :]))
        self.step(dve, dve.tensor_tensor(v(self.w), v(self.w), each(m[:, :], E0), ALU.mult))
        assert self.n == self.STEPS

    def pick(self, dve, values, out):
        v, m = self.v, self.m
        self.step(dve, dve.tensor_reduce(m[:, :], v(values), AX_X, ALU.max))
        self.step(dve, dve.tensor_tensor(v(self.eq), v(values), each(m[:, :], E0), ALU.is_ge))
        self.step(dve, dve.tensor_tensor(self.eq[:, :], self.eq[:, :], self.order[:, :], ALU.mult))
        self.step(dve, dve.tensor_reduce(m[:, :], v(self.eq), AX_X, ALU.max))
        self.step(dve, dve.tensor_tensor(v(out), v(self.eq), each(m[:, :], E0), ALU.is_ge))

    def scalar(self, act, logits_steps):
        act.wait_ge(self.sem, logits_steps)
        act.activation(self.pr[:, :], self.lg[:, :], ACT.Exp).then_inc(self.ex, 1)

    LOGITS = E0 + 3
    STEPS = LOGITS + 3 + 5 + 2 + 5 + 5


def load_and_normalise(nc, K):
    ps, ident, xnT = K.ps, K.ident, K.xnT
    with ExitStack() as ctx:
        x = ctx.enter_context(nc.sbuf_tensor("x_in", [P, N], F32))
        xn = ctx.enter_context(nc.sbuf_tensor("xn_tok", [P, N], F32))
        norm = Norm(ctx, nc, "n_in")
        sem = lambda n: ctx.enter_context(nc.semaphore(n))
        x_loaded = [sem(f"x_loaded{b}") for b in range(NB)]
        zeroed, xn_ready, xn_turned, xnT_ready = sem("ident_zeroed"), sem("xn_ready"), sem("xn_turned"), sem("xnT_ready")
        block = ctx.enter_context(nc.Block())

        @block.sync
        def _(sp):
            for b in range(NB):
                sp.dma_start(x[:, b * BLK:(b + 1) * BLK].rearrange("p (t d) -> p t d", d=D),
                             K.x[b * BLK:(b + 1) * BLK, :].rearrange("(t p) d -> p t d", p=P)).then_inc(x_loaded[b], 16)
            sp.dma_start(K.cols[:, :], K.cols_dram).then_inc(K.consts_loaded, 16)
            sp.dma_start(K.rows[:, :], K.rows_dram.broadcast_to([P, NROW])).then_inc(K.consts_loaded, 16)

        @block.gpsimd
        def _(pool):
            pool.memset(ident[:, :], 0.0).then_inc(zeroed, 1)
            pool.wait_ge(zeroed, 1)
            pool.affine_select(out=ident[:, :], in_=ident[:, :], compare_op=ALU.not_equal, fill=1.0,
                               base=0, pattern=[[-1, P]], channel_multiplier=1).then_inc(K.ident_ready, 1)

        @block.vector
        def _(dve):
            norm.vector(dve, x, lambda t: dve.wait_ge(x_loaded[t // TPB], 16))
            for t in range(NT):
                norm.apply(dve, xn, x, t, xn_ready)

        @block.tensor
        def _(pe):
            pe.wait_ge(K.ident_ready, 1)
            for t in range(NT):
                pe.wait_ge(xn_ready, t + 1)
                pe.transpose(ps[:, t // TPB, (t % TPB) * P:(t % TPB + 1) * P], xn[:, t * D:(t + 1) * D],
                             ident[:, :]).then_inc(xn_turned, 1)

        @block.scalar
        def _(act):
            norm.scalar(act)
            for b in range(NB):
                act.wait_ge(xn_turned, TPB * (b + 1))
                act.activation(xnT[:, b * BLK:(b + 1) * BLK], ps[:, b, :], ACT.Copy).then_inc(xnT_ready, 1)


def blk(t, b):
    return t[:, b * BLK:(b + 1) * BLK]


def gate_of_first_block(nc, K):
    ps, ident, xnT = K.ps, K.ident, K.xnT
    with ExitStack() as ctx:
        sb = lambda n, w: ctx.enter_context(nc.sbuf_tensor(n, [P, w], F32))
        sem = lambda n: ctx.enter_context(nc.semaphore(n))
        wv, wo, gw = sb("f0_wv", D), sb("f0_wo", D), sb("f0_gate_w", E0)
        b2 = ctx.enter_context(nc.sbuf_tensor("f0_b2", [E0, D], F32))
        cT = ctx.enter_context(nc.sbuf_tensor("f0_combineT", [E0, N], F32))
        vT, r1T, r1, x1, x1T, r2T, r2 = (sb(f"f0_{n}", N) for n in ("vT", "r1T", "r1", "x1", "x1T", "r2T", "r2"))
        w1 = [sb(f"f0_w1_{h}", FT0 * P) for h in range(2)]
        w2 = [sb(f"f0_w2_{h}", FT0 * D) for h in range(2)]
        b1 = [sb(f"f0_b1_{h}", FT0) for h in range(2)]
        cb = [sb(f"f0_weight_{h}", N) for h in range(2)]
        hr = sb("f0_hidden", 8 * BLK)
        hs = sb("f0_hidden_weighted", 8 * BLK)
        norm1, norm2, router = Norm(ctx, nc, "f0_n1"), Norm(ctx, nc, "f0_n2"), Router(ctx, nc, "f0")
        loaded = sem("f0_loaded")
        w_loaded = [sem(f"f0_w_loaded{h}") for h in range(2)]
        v_mm, v_ready, o_mm, r1T_ready = sem("f0_v_mm"), sem("f0_v_ready"), sem("f0_o_mm"), sem("f0_r1T_ready")
        r1_turned, r1_ready, x1_step, x1_ready = sem("f0_r1_turned"), sem("f0_r1_ready"), sem("f0_x1_step"), sem("f0_x1_ready")
        x1_turned, x1T_ready, logits_mm, routed = sem("f0_x1_turned"), sem("f0_x1T_ready"), sem("f0_logits_mm"), sem("f0_routed")
        c_turned, cT_ready, c_stored = sem("f0_c_turned"), sem("f0_cT_ready"), sem("f0_c_stored")
        h_mm, h_relu, h_weighted, y_mm = sem("f0_h_mm"), sem("f0_h_relu"), sem("f0_h_weighted"), sem("f0_y_mm")
        r2T_ready, r2_turned, r2_ready, x2_step, x2_ready, g_ready = (
            sem(f"f0_{n}") for n in ("r2T_ready", "r2_turned", "r2_ready", "x2_step", "x2_ready", "g_ready"))
        UE = NB * FT0
        block = ctx.enter_context(nc.Block())

        @block.sync
        def _(sp):
            sp.dma_start(wv[:, :], K.f0_wv).then_inc(loaded, 16)
            sp.dma_start(wo[:, :], K.f0_wo).then_inc(loaded, 16)
            sp.dma_start(gw[:, :], K.f0_gate_w).then_inc(loaded, 16)
            sp.dma_start(b2[:, :], K.f0_b2).then_inc(loaded, 16)

            def weights(e, half):
                sp.dma_start(w1[half][:, :], K.f0_w1[e]).then_inc(w_loaded[half], 16)
                sp.dma_start(w2[half][:, :], K.f0_w2[e]).then_inc(w_loaded[half], 16)
                sp.dma_start(b1[half][:, :], K.f0_b1[e]).then_inc(w_loaded[half], 16)

            def weighting(e, half):
                sp.dma_start(cb[half][:, :], K.combine_dram[e].broadcast_to([P, N])).then_inc(w_loaded[half], 16)

            for half in range(2):
                weights(half, half)
            sp.wait_ge(cT_ready, NB)
            sp.dma_start(K.combine_dram.rearrange("e o n -> (e o) n")[0:E0, :], cT[:, :]).then_inc(c_stored, 16)
            sp.wait_ge(c_stored, 16)
            for half in range(2):
                weighting(half, half)
            with sp.Fori(1, E0 // 2) as i:
                for half in range(2):
                    sp.wait_ge(y_mm, i * (2 * UE) + (half - 1) * UE)
                    weights(i * 2 + half, half)
                    weighting(i * 2 + half, half)

        @block.tensor
        def _(pe):
            pe.wait_ge(loaded, 64)
            for b in range(NB):
                pe.matmul(ps[:, b, :], wv[:, :], blk(xnT, b), start=True, stop=True).then_inc(v_mm, 1)
            for b in range(NB):
                pe.wait_ge(v_ready, b + 1)
                pe.matmul(ps[:, NB + b, :], wo[:, :], blk(vT, b), start=True, stop=True).then_inc(o_mm, 1)

            def turn(src, t, base, done):
                pe.transpose(ps[:, base + t // TPB, (t % TPB) * P:(t % TPB + 1) * P], src[:, t * P:(t + 1) * P],
                             ident[:, :]).then_inc(done, 1)

            for t in range(NT):
                pe.wait_ge(r1T_ready, t // TPB + 1)
                turn(r1T, t, 0, r1_turned)
            for t in range(NT):
                pe.wait_ge(x1_ready, t // TPB + 1)
                turn(x1, t, NB, x1_turned)
            for t in range(NT):
                pe.wait_ge(x1T_ready, t // TPB + 1)
                mm = pe.matmul(ps[:, 0, t * E0:(t + 1) * E0], x1T[:, t * P:(t + 1) * P], gw[:, :], start=True, stop=True)
            mm.then_inc(logits_mm, 1)
            pe.wait_ge(router.sem, Router.STEPS)
            for t in range(NT):
                pe.transpose(ps[0:E0, t // TPB, (t % TPB) * P:(t % TPB + 1) * P], router.w[:, t * E0:(t + 1) * E0],
                             ident[:, :]).then_inc(c_turned, 1)
            for b in range(NB):
                pe.wait_ge(cT_ready, b + 1)
                pe.matmul(ps[:, NB + b, :], b2[:, :], blk(cT, b), start=True, stop=True, skip_group_check=True)

            def out_product(u, half, b, ft):
                pe.wait_ge(h_weighted, u + 1)
                s = (b % 2) * FT0 + ft
                pe.matmul(ps[:, NB + b, :], w2[half][:, ft * D:(ft + 1) * D], blk(hs, s), start=False, stop=True,
                          skip_group_check=True).then_inc(y_mm, 1)

            def pair(i, first=False):
                base = i * (2 * UE)
                for half in range(2):
                    pe.wait_ge(w_loaded[half], i * 64 + 64)
                    for b in range(NB):
                        u0 = half * UE + b * FT0
                        for ft in range(FT0):
                            ge(pe, h_relu, base + (u0 + ft - FT0 + 1))
                            pe.matmul(ps[:, ft, :], w1[half][:, ft * P:(ft + 1) * P], blk(x1T, b),
                                      start=True, stop=True).then_inc(h_mm, 1)
                        if not (first and u0 == 0):
                            for ft in range(FT0):
                                out_product(base + (u0 - FT0 + ft), half if b else 1 - half, (b - 1) % NB, ft)

            pair(0, True)
            with pe.Fori(1, E0 // 2) as i:
                pair(i)
            for ft in range(FT0):
                out_product(E0 * UE - FT0 + ft, 1, NB - 1, ft)
            for t in range(NT):
                pe.wait_ge(r2T_ready, t // TPB + 1)
                turn(r2T, t, 0, r2_turned)

        @block.scalar
        def _(act):
            def copy_out(dst, done, ready, base, w=P):
                for b in range(NB):
                    act.wait_ge(ready, TPB * (b + 1))
                    act.activation(blk(dst, b), ps[0:w, base + b, :], ACT.Copy).then_inc(done, 1)

            act.wait_ge(K.consts_loaded, 32)
            for b in range(NB):
                act.wait_ge(v_mm, b + 1)
                act.activation(blk(vT, b), ps[:, b, :], ACT.Identity, bias=K.col(C_VB)).then_inc(v_ready, 1)
            copy_out(r1, r1_ready, r1_turned, 0)
            norm1.scalar(act)
            copy_out(x1T, x1T_ready, x1_turned, NB)
            router.scalar(act, Router.LOGITS)
            copy_out(cT, cT_ready, c_turned, 0, E0)

            def pair(i):
                base = i * (2 * UE)
                for half in range(2):
                    for b in range(NB):
                        for ft in range(FT0):
                            u = half * UE + b * FT0 + ft
                            act.wait_ge(h_mm, base + (u + 1))
                            ge(act, h_weighted, base + (u - 7))
                            act.activation(blk(hr, u % 8), ps[:, ft, :], ACT.Relu,
                                           bias=b1[half][:, ft:ft + 1]).then_inc(h_relu, 1)

            pair(0)
            with act.Fori(1, E0 // 2) as i:
                pair(i)
            copy_out(r2, r2_ready, r2_turned, 0)
            norm2.scalar(act)
            for b in range(NB):
                act.wait_ge(x2_ready, b + 1)
                act.activation(blk(K.g0, b), blk(r2T, b), ACT.Silu).then_inc(g_ready, 1)

        @block.vector
        def _(dve):
            dve.wait_ge(K.consts_loaded, 32)
            for b in range(NB):
                dve.wait_ge(o_mm, b + 1)
                dve.scalar_tensor_tensor(out=blk(r1T, b), in0=ps[:, NB + b, :], scalar=K.col(C_OUTB),
                                         in1=blk(xnT, b), op0=ALU.add, op1=ALU.add).then_inc(r1T_ready, 1)
            affine_norm(dve, K, norm1, r1, x1, r1_ready, x1_step, x1_ready, "ln1_g", "ln1_b")
            dve.wait_ge(logits_mm, 1)
            router.vector(dve, ps[:, 0, 0:NT * E0], K.row("gate_b"))

            def pair(i):
                base = i * (2 * UE)
                for half in range(2):
                    dve.wait_ge(w_loaded[half], i * 64 + 64)
                    for b in range(NB):
                        for ft in range(FT0):
                            u = half * UE + b * FT0 + ft
                            dve.wait_ge(h_relu, base + (u + 1))
                            ge(dve, y_mm, base + (u - 7))
                            dve.tensor_tensor(blk(hs, u % 8), blk(hr, u % 8), blk(cb[half], b),
                                              ALU.mult).then_inc(h_weighted, 1)

            pair(0)
            with dve.Fori(1, E0 // 2) as i:
                pair(i)
            dve.wait_ge(y_mm, E0 * UE)
            for b in range(NB):
                dve.tensor_tensor(blk(r2T, b), ps[:, NB + b, :], blk(x1T, b), ALU.add).then_inc(r2T_ready, 1)
            affine_norm(dve, K, norm2, r2, r2T, r2_ready, x2_step, x2_ready, "ln2_g", "ln2_b")


def affine_norm(dve, K, norm, src, dst, src_ready, step, done, g, b, count=0):
    norm.vector(dve, src, lambda t: dve.wait_ge(src_ready, t // TPB + 1))
    n = count
    for k in range(NB):
        for t in range(k * TPB, (k + 1) * TPB):
            norm.apply(dve, dst, src, t, step)
        n += TPB
        tiles = blk(dst, k).rearrange("p (t d) -> p t d", d=D)
        dve.wait_ge(step, n)
        dve.tensor_tensor(tiles, tiles, spread(K.row(g), TPB), ALU.mult).then_inc(step, 1)
        n += 1
        dve.wait_ge(step, n)
        dve.tensor_tensor(tiles, tiles, spread(K.row(b), TPB), ALU.add).then_inc(done, 1)


class Kit:

    def col(self, c):
        return self.cols[:, c:c + 1]

    def row(self, name):
        at, w = ROWS[name]
        return self.rows[:, at:at + w]


STEPS = NB * NT
LAG = 3
SB = 3
PBUF = 5
O_BANK = 3
M_BANK = 5
W_BANK = 7
MU = NT * NB
ON_VECTOR = (1, 4, 7, 10, 13)
NV = len(ON_VECTOR)
PROJ = {0: ("K", 0), 1: ("K", 1), 2: ("K", 2), 3: ("K", 3), 4: ("Q", 0), 5: ("Q", 1), 7: ("Q", 2), 9: ("Q", 3)}
ROWS_AT = {43: ("N", 0), 63: ("N", 1)}
TOPS_AT = {41: 0, 62: 1}
TURN = ({6: ("T", 3), 8: ("W", 3)},
        {22: ("T", 0), 24: ("W", 0), 39: ("T", 1), 41: ("W", 1), 54: ("T", 2), 56: ("W", 2)})
MAX_FROM, MAX_TO = 9, 60


def max_units(k):
    done = lambda j: max(0, min(MU, (j - MAX_FROM) * MU // (MAX_TO - MAX_FROM)))
    return range(done(k), done(k + 1))


def before(k, n):
    return k - n + 1 if k >= n else next(j + 1 for j in range(-1, -STEPS, -1) if (j + STEPS) % n == k)


def lower_on_vector(mt):
    return mt in ON_VECTOR


def lower_count(k, on_vector):
    full, part = divmod(k, NT)
    n = sum(lower_on_vector(m) == on_vector for m in range(part))
    return full * (NV if on_vector else NT - NV) + n


def attention_of_first_block(nc, K):
    ps, ident, xnT, yT = K.ps, K.ident, K.xnT, K.yT
    bank = lambda b: ps[:, b, :]
    values = K.values[:, :].rearrange("p (t h w) -> p t h w", t=NT, h=H)
    with ExitStack() as ctx:
        sb = lambda n, w: ctx.enter_context(nc.sbuf_tensor(n, [P, w], F32))
        sem = lambda n: ctx.enter_context(nc.semaphore(n))
        wv, bv, v32 = sb("a0_wv", H * HD), sb("a0_bv", H * HD), sb("a0_v32", 4 * BLK)
        loaded, v_mm, v_sum, v_high, v_low, ones = (
            sem(f"a0_{n}") for n in ("v_loaded", "v_mm", "v_sum", "v_high", "v_low", "v_ones"))
        UNITS = NT * 2
        block = ctx.enter_context(nc.Block())

        @block.sync
        def _(sp):
            sp.dma_start(wv[:, :], K.a0_wv).then_inc(loaded, 16)
            sp.dma_start(bv[:, :], K.a0_bv.broadcast_to([P, H * HD])).then_inc(loaded, 16)

        @block.tensor
        def _(pe):
            pe.wait_ge(loaded, 32)
            for u in range(UNITS):
                t, half = divmod(u, 2)
                ge(pe, v_sum, u - 7)
                pe.matmul(bank(u % 8), xnT[:, t * P:(t + 1) * P], blk(wv, half), start=True, stop=True).then_inc(v_mm, 1)

        def part(u, first):
            t, half = divmod(u, 2)
            return values[:, t, half * 8:half * 8 + 8, first:first + HD]

        def source(u):
            return blk(v32, u % 4).rearrange("p (h d) -> p h d", d=HD)

        @block.vector
        def _(dve):
            dve.memset(values[:, :, :, HD], 1.0).then_inc(ones, 1)
            dve.tensor_scalar(yT[:, :], xnT[:, :], K.col(C_BO), None, ALU.add).then_inc(ones, 1)
            dve.wait_ge(loaded, 32)
            for u in range(UNITS):
                dve.wait_ge(v_mm, u + 1)
                ge(dve, v_low, u - 3)
                dve.tensor_tensor(blk(v32, u % 4), bank(u % 8), blk(bv, u % 2), ALU.add).then_inc(v_sum, 1)
                if u:
                    dve.wait_ge(v_high, u)
                    dve.tensor_tensor(part(u - 1, HD + 1), source(u - 1), part(u - 1, 0), ALU.subtract).then_inc(v_low, 1)
            dve.wait_ge(v_high, UNITS)
            dve.tensor_tensor(part(UNITS - 1, HD + 1), source(UNITS - 1), part(UNITS - 1, 0), ALU.subtract).then_inc(v_low, 1)

        @block.scalar
        def _(act):
            for u in range(UNITS):
                act.wait_ge(v_sum, u + 1)
                act.activation(part(u, 0), source(u), ACT.Copy).then_inc(v_high, 1)

    with ExitStack() as ctx:
        sb = lambda n, w, dt=F32, p=P: ctx.enter_context(nc.sbuf_tensor(n, [p, w], dt))
        sem = lambda n: ctx.enter_context(nc.semaphore(n))
        two = lambda n, w, dt=F32: [sb(f"{n}{s}", w, dt) for s in range(2)]
        q_stack, k_stack = two("q_stack", N, F32R), two("k_stack", N, F32R)
        q_row, k_low = two("q_row", N, F32R), two("k_low", N, F32R)
        v_head = two("v_head", NT * VW, F16)
        w_qk = two("w_qk", 2 * P)
        head_cols = two("head_cols", 3)
        q_cols = two("q_cols", 2)
        wo = sb("a0_wo", D)
        qk32 = two("qk32_", BLK)
        maxima, top = sb("maxima", MU), sb("top", NT)
        row = ctx.enter_context(nc.sbuf_tensor("minus_max", [NT // 2, 2 * P], F32R))
        prob, prob_low = sb("prob", PBUF * BLK), sb("prob_low", PBUF * BLK, F16)
        o_low, o_sum, o_rz = sb("o_low", TPB * HD), sb("o_sum", TPB * HD), sb("o_rz", TPB)
        ctxt = sb("contexts", NT * P)
        ctxT = sb("contextsT", BLK)
        prob_high = prob[:, :].bitcast(BF16).rearrange("p (n two) -> p n two", two=2)[:, :, 1]
        O = ps[:, O_BANK:O_BANK + 2, 0:2 * VW].rearrange("p b (j w) -> p b j w", w=VW)

        w_loaded = [sem(f"qk_w_loaded{s}") for s in range(2)]
        wo_loaded, k_ones = sem("wo_loaded"), sem("k_ones")
        row_sent = [sem(f"row_sent{n}") for n in range(2)]
        cols_step = sem("q_cols_step")
        job_ready, job_done = sem("job_ready"), sem("job_done")
        qk_rounded, qk_split = sem("qk_rounded"), sem("qk_split")
        max_mm, max_taken, top_ready = sem("max_mm"), sem("max_taken"), sem("top_ready")
        v_moved = sem("v_moved")
        scored, exp_done, low_pool, low_vector, pv_done = (
            sem(n) for n in ("scored", "exp_done", "low_pool", "low_vector", "pv_done"))
        o_low_copied, o_free, o_summed, ctx_ready = sem("o_low_copied"), sem("o_free"), sem("o_summed"), sem("ctx_ready")
        o_rz_ready = sem("o_rz_ready")
        block = ctx.enter_context(nc.Block())

        class Half:

            def __init__(self, i, s, main=True, prep=True):
                self.i, self.s, self.main, self.prep = i, s, main, prep
                self.pair = Count(i, 1, 0)
                self.h = Count(i, 2, s) if main else Count(0, 0, -1)
                self.g = self.h + 1
                jobs = {}
                if prep:
                    jobs |= PROJ | ROWS_AT
                if main:
                    jobs |= TURN[s]
                if main and isinstance(i, int) and i == 0 and s == 0:
                    jobs = {k: j for k, j in jobs.items() if k not in TURN[0]}
                self.jobs = dict(sorted(jobs.items()))
                before = sorted(self.jobs)
                self.index = {k: n for n, k in enumerate(before)}
                self.weights = Count(i, 1, s) if main else Count(0, 0, 0)
                self.start = isinstance(i, int) and i == 0 and s == 0
                self.end = isinstance(i, int) and i == H // 2 - 1
                if not main:
                    self.job0 = Count(0, 0, 0)
                elif isinstance(i, int) and i == 0:
                    self.job0 = Count(0, 0, 10 if s == 0 else 20)
                else:
                    self.job0 = Count(i, 28, 8 if s == 0 else 20)

            def job(self, k):
                return self.job0 + self.index[k]

        def run(eng, body):
            body(Half(0, 1, main=False))
            for s in range(2):
                body(Half(0, s))
            with eng.Fori(1, H // 2 - 1) as i:
                BASES.clear()
                for s in range(2):
                    body(Half(i, s))
            BASES.clear()
            body(Half(H // 2 - 1, 0))
            body(Half(H // 2 - 1, 1, prep=False))

        def lower(eng, x, k, done):
            ge(eng, exp_done, x.h * STEPS + (k + 1))
            ge(eng, pv_done, x.h * STEPS + before(k, PBUF))
            eng.tensor_tensor(blk(prob_low, k % PBUF), blk(prob, k % PBUF), blk(prob_high, k % PBUF),
                              ALU.subtract).then_inc(done, 1)

        def tail():
            x = Half(H // 2, 0, prep=False)
            x.job0 = Count(0, 0, (H // 2 - 1) * 28 + 26)
            return x

        @block.sync
        def _(sp):
            def load(h, s):
                sp.dma_start(w_qk[s][:, :], K.a0_wqk[h.value()]).then_inc(w_loaded[s], 16)
                sp.dma_start(head_cols[s][:, :], K.a0_cols[h.value()]).then_inc(w_loaded[s], 16)

            def load_wo(i):
                sp.dma_start(wo[:, :], K.a0_wo[i.value()]).then_inc(wo_loaded, 16)

            load(Count(0, 0, 0), 0)
            load(Count(0, 0, 1), 1)
            load_wo(Count(0, 0, 0))

            def body(x):
                if x.main and not x.end:
                    ge(sp, qk_split, x.h * 8 + 8)
                    load(x.h + 2, x.s)
                if x.main and x.s == 0 and not x.start:
                    ge(sp, job_ready, x.job(8) + 1)
                    load_wo(x.pair)
                if x.prep:
                    for k, (_, n) in ROWS_AT.items():
                        ge(sp, job_done, x.job(k) + 1)
                        sp.dma_start(q_row[1 - x.s][HD:HD + 1, n * 2 * BLK:(n + 1) * 2 * BLK].bitcast(F32),
                                     row[:, n * P:(n + 1) * P].bitcast(F32)).then_inc(row_sent[n], 16)

            run(sp, body)

        @block.tensor
        def _(pe):
            def pv(x, k):
                own = k >= 0
                h, s, k = (x.h, x.s, k) if own else (x.h - 1, 1 - x.s, k + STEPS)
                nb, mt = divmod(k, NT)
                if lower_on_vector(mt):
                    ge(pe, low_vector, h * (NB * NV) + lower_count(k + 1, True))
                else:
                    ge(pe, low_pool, h * (NB * (NT - NV)) + lower_count(k + 1, False))
                if mt == 0:
                    ge(pe, o_free, h * NB + nb)
                    if nb == 0:
                        ge(pe, v_moved, h + 1)
                at = k % PBUF * BLK
                buf = lambda t, j: t[:, at + j * P:at + (j + 1) * P]
                v = v_head[s][:, mt * VW:(mt + 1) * VW]
                for j in range(TPB):
                    o = O[:, j // 2, j % 2, :]
                    pe.matmul(o, buf(prob_high, j), v, start=(mt == 0 and j % 2 == 0), stop=False, skip_group_check=True)
                    mm = pe.matmul(o[:, 0:HD + 1], buf(prob_low, j), v[:, 0:HD + 1], start=False, stop=(mt == NT - 1),
                                   skip_group_check=True)
                mm.then_inc(pv_done, 1)

            def job(x, k):
                kind, n = x.jobs[k]
                ge(pe, job_done, x.job(k))
                nxt = 1 - x.s
                if kind in "KQ":
                    if (kind, n) == ("K", 0):
                        ge(pe, w_loaded[nxt], x.weights * 32 + 32)
                    c = 0 if kind == "Q" else P
                    pe.matmul(bank(W_BANK), w_qk[nxt][:, c:c + P], blk(xnT, n), start=True,
                              stop=True).then_inc(job_ready, 1)
                elif kind == "N":
                    ge(pe, top_ready, x.g * 2 + (n + 1))
                    pe.transpose(ps[0:NT // 2, W_BANK, 0:P], top[:, n * 8:(n + 1) * 8], ident[:, :]).then_inc(job_ready, 1)
                elif kind == "T":
                    ge(pe, ctx_ready, x.h * NB + (n + 1 if x.s else 0))
                    for j in range(TPB):
                        mm = pe.transpose(ps[:, W_BANK, j * P:(j + 1) * P],
                                          ctxt[:, (n * TPB + j) * P:(n * TPB + j + 1) * P], ident[:, :])
                    mm.then_inc(job_ready, 1)
                else:
                    ge(pe, wo_loaded, x.pair * 16 + 16 * x.s)
                    pe.matmul(bank(W_BANK), wo[:, :], ctxT[:, :], start=True, stop=True).then_inc(job_ready, 1)

            def body(x):
                cur, nxt = x.s, 1 - x.s
                for k in range(STEPS):
                    nb, mt = divmod(k, NT)
                    if x.main:
                        if k == 0:
                            ge(pe, qk_split, x.h * 8 + 8)
                        if k % (2 * NT) == 0:
                            ge(pe, row_sent[nb // 2], x.h * 16 + 16)
                        ge(pe, exp_done, x.h * STEPS + before(k, SB))
                        m = slice(mt * P, (mt + 1) * P)
                        pe.matmul(bank(k % SB), k_stack[cur][:, m], blk(q_stack[cur], nb), start=True, stop=False)
                        pe.matmul(bank(k % SB), k_low[cur][0:HD + 1, m], blk(q_row[cur], nb)[0:HD + 1, :], start=False,
                                  stop=True).then_inc(scored, 1)
                    if k in x.jobs:
                        job(x, k)
                    if x.prep:
                        for u in max_units(k):
                            nt, mb = divmod(u, NB)
                            if u == 0:
                                ge(pe, qk_split, x.g * 8 + 5)
                            elif mb == 0 and nt % TPB == 0:
                                ge(pe, qk_split, x.g * 8 + (5 + nt // TPB))
                            ge(pe, max_taken, x.g * MU + (u - 1))
                            pe.matmul(bank(M_BANK + u % 2), q_stack[nxt][:, nt * P:(nt + 1) * P], blk(k_stack[nxt], mb),
                                      start=True, stop=True).then_inc(max_mm, 1)
                    if x.main and not (k < LAG and x.start):
                        pv(x, k - LAG)
                if x.main and not x.prep:
                    for k in range(STEPS, STEPS + LAG):
                        pv(x, k - LAG)

            ge(pe, k_ones, 2)
            run(pe, body)
            for k in TURN[0]:
                job(tail(), k)

        @block.scalar
        def _(act):
            def low_contexts(h, nb):
                ge(act, pv_done, h * STEPS + (nb + 1) * NT)
                ge(act, o_free, h * NB + nb)
                act.activation(o_low[:, :].rearrange("p (b j w) -> p b j w", b=2, j=2), O[:, :, :, HD + 1:VW],
                               ACT.Copy).then_inc(o_low_copied, 1)

            def job(x, k):
                kind, n = x.jobs[k]
                if kind == "W":
                    return
                ge(act, job_ready, x.job(k) + 1)
                nxt = 1 - x.s
                if kind == "K":
                    ge(act, qk_split, x.g * 8 + (n - 1))
                    act.activation(qk32[n % 2][:, :], bank(W_BANK), ACT.Identity, bias=head_cols[nxt][:, 1:2]).then_inc(job_done, 1)
                elif kind == "Q":
                    ge(act, cols_step, x.g * 2 + 2)
                    ge(act, qk_split, x.g * 8 + (NB + n - 1))
                    act.activation(qk32[n % 2][:, :], bank(W_BANK), ACT.Identity, bias=q_cols[nxt][:, 1:2],
                                   scale=q_cols[nxt][:, 0:1])
                    act.activation(blk(q_row[nxt], n)[0:HD, :], ps[0:HD, W_BANK, :], ACT.Identity,
                                   bias=q_cols[nxt][0:HD, 1:2], scale=q_cols[nxt][0:HD, 0:1]).then_inc(job_done, 1)
                elif kind == "N":
                    ge(act, row_sent[n], x.g * 16)
                    act.activation(row[:, n * P:(n + 1) * P], ps[0:NT // 2, W_BANK, 0:P], ACT.Copy,
                                   scale=-1.0).then_inc(job_done, 1)
                else:
                    act.activation(ctxT[:, :], bank(W_BANK), ACT.Copy).then_inc(job_done, 1)

            def body(x):
                for k in range(STEPS):
                    if x.main:
                        ge(act, scored, x.h * STEPS + (k + 1))
                        ge(act, pv_done, x.h * STEPS + before(k, PBUF))
                        act.activation(blk(prob, k % PBUF), bank(k % SB), ACT.Exp).then_inc(exp_done, 1)
                        if k % NT == LAG - 1:
                            if k >= NT:
                                low_contexts(x.h, k // NT - 1)
                            elif not x.start:
                                low_contexts(x.h - 1, NB - 1)
                    if k in x.jobs:
                        job(x, k)

            run(act, body)
            low_contexts(Count(0, 0, H - 1), NB - 1)
            for k in TURN[0]:
                job(tail(), k)

        @block.gpsimd
        def _(pool):
            for s in range(2):
                pool.memset(k_low[s][HD:HD + 1, :].bitcast(F32), 1.0).then_inc(k_ones, 1)

            def body(x):
                if x.main:
                    for k in range(STEPS):
                        if not lower_on_vector(k % NT):
                            lower(pool, x, k, low_pool)

            run(pool, body)

        @block.vector
        def _(dve):
            def contexts(h, s, nb):
                ge(dve, o_low_copied, h * NB + (nb + 1))
                rz = o_rz[:, :].rearrange("p (b j) -> p b j", j=2)
                dve.reciprocal(rz, O[:, :, :, HD]).then_inc(o_rz_ready, 1)
                dve.tensor_tensor(o_sum[:, :].rearrange("p (b j w) -> p b j w", b=2, j=2), O[:, :, :, 0:HD],
                                  o_low[:, :].rearrange("p (b j w) -> p b j w", b=2, j=2), ALU.add).then_inc(o_free, 1)
                ge(dve, o_free, h * NB + (nb + 1))
                dst = ctxt[:, :].rearrange("p (t w) -> p t w", w=P)[:, nb * TPB:(nb + 1) * TPB, s * HD:(s + 1) * HD]
                ge(dve, o_rz_ready, h * NB + (nb + 1))
                dve.tensor_tensor(dst, o_sum[:, :].rearrange("p (t w) -> p t w", w=HD), each(o_rz[:, :], HD),
                                  ALU.mult).then_inc(ctx_ready, 1)

            def job(x, k):
                kind, n = x.jobs[k]
                nxt = 1 - x.s
                if kind in "KQ":
                    m = n + (NB if kind == "Q" else 0)
                    ge(dve, job_done, x.job(k) + 1)
                    stack = blk((k_stack if kind == "K" else q_stack)[nxt], n)
                    dve.tensor_copy(stack, qk32[n % 2][:, :]).then_inc(qk_rounded, 1)
                    ge(dve, qk_rounded, x.g * 8 + (m + 1))
                    if kind == "K":
                        dst, rows = blk(k_low[nxt], n)[0:HD, :], slice(0, HD)
                    else:
                        dst, rows = stack[HD:P, :], slice(HD, P)
                    dve.tensor_tensor(dst, qk32[n % 2][rows, :], stack.bitcast(F32)[rows, :],
                                      ALU.subtract).then_inc(qk_split, 1)
                elif kind == "W":
                    ge(dve, job_ready, x.job(k) + 1)
                    dve.tensor_tensor(blk(yT, n), blk(yT, n), bank(W_BANK), ALU.add).then_inc(job_done, 1)

            def body(x):
                nxt = 1 - x.s
                for k in range(STEPS):
                    if x.prep and k == 0:
                        ge(dve, w_loaded[nxt], x.weights * 32 + 32)
                        dve.tensor_scalar(q_cols[nxt][:, 0:1], head_cols[nxt][:, 2:3], float(HD) ** -0.5, None,
                                          ALU.mult).then_inc(cols_step, 1)
                        ge(dve, cols_step, x.g * 2 + 1)
                        dve.tensor_tensor(q_cols[nxt][:, 1:2], head_cols[nxt][:, 0:1], q_cols[nxt][:, 0:1],
                                          ALU.mult).then_inc(cols_step, 1)
                    if x.main and k % NT == LAG:
                        if k >= NT:
                            contexts(x.h, x.s, k // NT - 1)
                        elif not x.start:
                            contexts(x.h - 1, 1 - x.s, NB - 1)
                    if x.main and lower_on_vector((k - 1) % NT):
                        lower(dve, x, k - 1, low_vector)
                    if k - 1 in x.jobs:
                        job(x, k - 1)
                    if x.prep:
                        for u in max_units(k):
                            ge(dve, max_mm, x.g * MU + (u + 1))
                            dve.reduce_max(maxima[:, u:u + 1], bank(M_BANK + u % 2), AX_X).then_inc(max_taken, 1)
                        if k in TOPS_AT:
                            n = TOPS_AT[k]
                            ge(dve, max_taken, x.g * MU + (n + 1) * MU // 2)
                            dve.tensor_reduce(top[:, n * 8:(n + 1) * 8], maxima[:, n * MU // 2:(n + 1) * MU // 2].rearrange(
                                "p (t b) -> p t b", b=NB), AX_X, ALU.max).then_inc(top_ready, 1)
                        if k == 8:
                            if x.main:
                                ge(dve, pv_done, x.h * STEPS)
                            head = (x.h + 1).value()
                            dve.tensor_copy(v_head[nxt][:, :].rearrange("p (t w) -> p t w", w=VW),
                                            values[:, :, head, :]).then_inc(v_moved, 1)

            run(dve, body)
            contexts(Count(0, 0, H - 1), 1, NB - 1)
            for k in TURN[0]:
                job(tail(), k)


def end_of_first_block(nc, K):
    ps, ident = K.ps, K.ident
    with ExitStack() as ctx:
        sb = lambda n, w: ctx.enter_context(nc.sbuf_tensor(n, [P, w], F32))
        sem = lambda n: ctx.enter_context(nc.semaphore(n))
        x, y, s, xn = sb("d_x", N), sb("d_y", N), sb("d_s", N), sb("d_xn", N)
        norm_y, norm_x = Norm(ctx, nc, "d_ny"), Norm(ctx, nc, "d_nx")
        x_loaded, y_turned, y_ready, s_step, s_ready, gated, x1_ready, xn_ready, xn_turned, xn1T_ready = (
            sem(f"d_{n}") for n in ("x_loaded", "y_turned", "y_ready", "s_step", "s_ready", "gated", "x1_ready",
                                    "xn_ready", "xn_turned", "xn1T_ready"))
        block = ctx.enter_context(nc.Block())

        @block.sync
        def _(sp):
            sp.dma_start(x[:, :].rearrange("p (t d) -> p t d", d=D),
                         K.x.rearrange("(t p) d -> p t d", p=P)).then_inc(x_loaded, 16)

        @block.tensor
        def _(pe):
            def turn(src, t, base, done):
                pe.transpose(ps[:, base + t // TPB, (t % TPB) * P:(t % TPB + 1) * P], src[:, t * P:(t + 1) * P],
                             ident[:, :]).then_inc(done, 1)

            for t in range(NT):
                turn(K.yT, t, 0, y_turned)
            for t in range(NT):
                pe.wait_ge(xn_ready, t + 1)
                turn(xn, t, NB, xn_turned)

        @block.scalar
        def _(act):
            for b in range(NB):
                act.wait_ge(y_turned, TPB * (b + 1))
                act.activation(blk(y, b), ps[:, b, :], ACT.Copy).then_inc(y_ready, 1)
            norm_y.scalar(act)
            norm_x.scalar(act)
            for b in range(NB):
                act.wait_ge(xn_turned, TPB * (b + 1))
                act.activation(blk(K.xn1T, b), ps[:, NB + b, :], ACT.Copy).then_inc(xn1T_ready, 1)

        @block.vector
        def _(dve):
            affine_norm(dve, K, norm_y, y, s, y_ready, s_step, s_ready, "gamma", "beta")
            dve.wait_ge(x_loaded, 16)
            for b in range(NB):
                dve.wait_ge(s_ready, b + 1)
                dve.tensor_tensor(blk(s, b), blk(s, b), blk(K.g0, b), ALU.mult).then_inc(gated, 1)
            for b in range(NB):
                dve.wait_ge(gated, b + 1)
                dve.tensor_tensor(blk(K.x1, b), blk(s, b), blk(x, b), ALU.add).then_inc(x1_ready, 1)
            norm_x.vector(dve, K.x1, lambda t: dve.wait_ge(x1_ready, t // TPB + 1))
            for t in range(NT):
                norm_x.apply(dve, xn, K.x1, t, xn_ready)


def widths(mt, nb):
    return max(0, mt - nb * TPB) * P


def second_block(nc, K):
    ps, ident, xT = K.ps, K.ident, K.xn1T
    SCALE = float(D) ** -0.5
    tiles = [(mt, nb) for mt in range(NT) for nb in range(mt // TPB, NB)]
    place = {}
    at = 0
    for tile in tiles:
        place[tile] = at
        at += BLK - widths(*tile)
    SW, NTILES = at, len(tiles)
    with ExitStack() as ctx:
        sb = lambda n, w: ctx.enter_context(nc.sbuf_tensor(n, [P, w], F32))
        sem = lambda n: ctx.enter_context(nc.semaphore(n))
        wq, wk, wv, gw = sb("a1_wq", D), sb("a1_wk", D), sb("a1_wv", D), sb("f1_router_w", E0)
        with ExitStack() as inner:
            qT, kT, v = (inner.enter_context(nc.sbuf_tensor(f"a1_{n}", [P, N], F32)) for n in ("qT", "kT", "v"))
            S = inner.enter_context(nc.sbuf_tensor("a1_scores", [P, SW], F32))
            maxima, sums = (inner.enter_context(nc.sbuf_tensor(f"a1_{n}", [P, NTILES], F32)) for n in ("maxima", "sums"))
            small = inner.enter_context(nc.sbuf_tensor("a1_small", [P, 8], F32))
            ones = inner.enter_context(nc.sbuf_tensor("a1_ones", [P, P], F32))
            loaded, q_mm, q_ready, v_mm, v_ready = (sem(f"a1_{n}") for n in ("loaded", "q_mm", "q_ready", "v_mm", "v_ready"))
            s_mm, s_copied, s_masked, s_maxed, m_step, m_turned, m_spread, m_ready = (
                sem(f"a1_{n}") for n in ("s_mm", "s_copied", "s_masked", "s_maxed", "m_step", "m_turned", "m_spread", "m_ready"))
            e_done, z_ready, z_spread, rz_ready, pv_mm, s_ready, ones_ready = (
                sem(f"a1_{n}") for n in ("e_done", "z_ready", "z_spread", "rz_ready", "pv_mm", "s_ready", "ones_ready"))
            scores = lambda mt, nb: S[:, place[mt, nb]:place[mt, nb] + BLK - widths(mt, nb)]
            diagonal = [t for t in tiles if t[0] // TPB == t[1]]
            block = inner.enter_context(nc.Block())

            @block.sync
            def _(sp):
                for dst, src in ((wq, K.a1_wq), (wk, K.a1_wk), (wv, K.a1_wv), (gw, K.f1_router_w)):
                    sp.dma_start(dst[:, :], src).then_inc(loaded, 16)

            @block.tensor
            def _(pe):
                pe.wait_ge(loaded, 64)
                for n in range(2 * NB):
                    pe.matmul(ps[:, n, :], (wq, wk)[n // NB][:, :], blk(xT, n % NB), start=True, stop=True).then_inc(q_mm, 1)
                for t in range(NT):
                    pe.wait_ge(q_ready, t // TPB + 1)
                    pe.matmul(ps[:, t // TPB, (t % TPB) * P:(t % TPB + 1) * P], xT[:, t * P:(t + 1) * P], wv[:, :],
                              start=True, stop=True).then_inc(v_mm, 1)
                pe.wait_ge(q_ready, 2 * NB)
                for n, (mt, nb) in enumerate(tiles):
                    w = widths(mt, nb)
                    ge(pe, s_copied, n - 3)
                    pe.matmul(ps[:, NB + n % 4, w:BLK], kT[:, mt * P:(mt + 1) * P], qT[:, nb * BLK + w:(nb + 1) * BLK],
                              start=True, stop=True).then_inc(s_mm, 1)
                pe.wait_ge(s_copied, NTILES)
                pe.wait_ge(m_step, 1)
                pe.transpose(ps[0:1, NB, 0:P], small[:, 0:1], ident[:, :]).then_inc(m_turned, 1)
                pe.wait_ge(m_step, 2)
                pe.wait_ge(ones_ready, 1)
                pe.matmul(ps[:, NB + 1, 0:1], ones[0:1, :], small[0:1, 1:2], start=True, stop=True).then_inc(m_spread, 1)
                pe.wait_ge(v_ready, NB)
                for mt in range(NT):
                    for nb in range(mt // TPB, NB):
                        w = widths(mt, nb)
                        pe.wait_ge(e_done, tiles.index((mt, nb)) + 1)
                        mm = pe.matmul(ps[:, nb, w:BLK], v[:, mt * P:(mt + 1) * P], scores(mt, nb), start=(mt == 0),
                                       stop=(mt == nb * TPB + TPB - 1), skip_group_check=True)
                    if mt % TPB == TPB - 1:
                        mm.then_inc(pv_mm, 1)
                pe.wait_ge(z_ready, 1)
                pe.matmul(ps[:, NB + 2, 0:1], ones[:, :], small[:, 4:5], start=True, stop=True).then_inc(z_spread, 1)

            @block.gpsimd
            def _(pool):
                pool.memset(ones[:, :], 1.0).then_inc(ones_ready, 1)
                for mt, nb in diagonal:
                    pool.wait_ge(s_copied, tiles.index((mt, nb)) + 1)
                    s = scores(mt, nb)[:, 0:P]
                    pool.affine_select(out=s, in_=s, compare_op=ALU.is_ge, fill=-BIG, base=0, pattern=[[1, P]],
                                       channel_multiplier=-1).then_inc(s_masked, 1)

            @block.scalar
            def _(act):
                act.wait_ge(q_mm, 1)
                for n in range(2 * NB):
                    act.wait_ge(q_mm, n + 1)
                    act.activation(blk((qT, kT)[n // NB], n % NB), ps[:, n, :], ACT.Identity,
                                   bias=K.col((C_Q1B, C_K1B)[n // NB])).then_inc(q_ready, 1)
                for n, (mt, nb) in enumerate(tiles):
                    act.wait_ge(s_mm, n + 1)
                    act.activation(scores(mt, nb), ps[:, NB + n % 4, widths(mt, nb):BLK], ACT.Copy).then_inc(s_copied, 1)
                act.wait_ge(m_spread, 1)
                act.activation(small[:, 2:3], ps[:, NB + 1, 0:1], ACT.Copy, scale=-SCALE).then_inc(m_ready, 1)
                act.wait_ge(m_ready, 1)
                act.wait_ge(s_masked, len(diagonal))
                act.wait_ge(s_maxed, NTILES)
                for n, (mt, nb) in enumerate(tiles):
                    act.activation(scores(mt, nb), scores(mt, nb), ACT.Exp, bias=small[:, 2:3], scale=SCALE,
                                   accum_out=sums[:, n:n + 1]).then_inc(e_done, 1)

            @block.vector
            def _(dve):
                for b in range(NB):
                    dve.wait_ge(v_mm, TPB * (b + 1))
                    dve.tensor_tensor(blk(v, b).rearrange("p (t d) -> p t d", d=D),
                                      ps[:, b, :].rearrange("p (t d) -> p t d", d=D),
                                      spread(K.row("v1b"), TPB), ALU.add).then_inc(v_ready, 1)
                for n, (mt, nb) in enumerate(tiles):
                    if (mt, nb) in diagonal:
                        dve.wait_ge(s_masked, diagonal.index((mt, nb)) + 1)
                    dve.wait_ge(s_copied, n + 1)
                    dve.reduce_max(maxima[:, n:n + 1], scores(mt, nb), AX_X).then_inc(s_maxed, 1)
                dve.wait_ge(s_maxed, NTILES)
                dve.reduce_max(small[:, 0:1], maxima[:, :], AX_X).then_inc(m_step, 1)
                dve.wait_ge(m_turned, 1)
                dve.reduce_max(small[0:1, 1:2], ps[0:1, NB, 0:P], AX_X).then_inc(m_step, 1)
                dve.wait_ge(e_done, NTILES)
                dve.reduce_sum(small[:, 4:5], sums[:, :], AX_X).then_inc(z_ready, 1)
                dve.wait_ge(z_spread, 1)
                dve.reciprocal(small[:, 5:6], ps[:, NB + 2, 0:1]).then_inc(rz_ready, 1)
                dve.wait_ge(rz_ready, 1)
                for b in range(NB):
                    dve.wait_ge(pv_mm, b + 1)
                    dve.tensor_scalar(blk(K.sT, b), ps[:, b, :], small[:, 5:6], None, ALU.mult).then_inc(s_ready, 1)

        w1 = [sb(f"f1_w1_{h}", FT1 * P) for h in range(2)]
        w3 = [sb(f"f1_w3_{h}", FT1 * P) for h in range(2)]
        w2 = [sb(f"f1_w2_{h}", FT1 * D) for h in range(2)]
        cb = [sb(f"f1_weight_{h}", N) for h in range(2)]
        SLOTS = 8
        hg, hu, hs = sb("f1_gate", SLOTS * BLK), sb("f1_product", SLOTS * BLK), sb("f1_hidden", SLOTS * BLK)
        cT = ctx.enter_context(nc.sbuf_tensor("f1_combineT", [E0, N], F32))
        one_row = ctx.enter_context(nc.sbuf_tensor("f1_one", [1, N], F32))
        g1 = sb("f1_g", N)
        o = sb("f1_out", N)
        router = Router(ctx, nc, "f1")
        w_loaded = [sem(f"f1_w_loaded{h}") for h in range(2)]
        logits_mm, c_turned, cT_ready, one_ready, c_stored = (
            sem(f"f1_{n}") for n in ("logits_mm", "c_turned", "cT_ready", "one_ready", "c_stored"))
        h_mm, h_gated, h_mult, h_ready, y_mm, g_ready, p_ready, p_turned, o_ready, o_stored = (
            sem(f"f1_{n}") for n in ("h_mm", "h_gated", "h_mult", "h_ready", "y_mm", "g_ready", "p_ready",
                                     "p_turned", "o_ready", "o_stored"))
        UE = NB * FT1
        block = ctx.enter_context(nc.Block())

        @block.sync
        def _(sp):
            def weights(e, s):
                sp.dma_start(w1[s][:, :], K.f1_w1[e]).then_inc(w_loaded[s], 16)
                sp.dma_start(w3[s][:, :], K.f1_w3[e]).then_inc(w_loaded[s], 16)
                sp.dma_start(w2[s][:, :].rearrange("p (k d) -> p k d", d=D),
                             K.f1_w2[e].rearrange("(k p) d -> p k d", p=P)).then_inc(w_loaded[s], 16)

            def weighting(e, s):
                sp.dma_start(cb[s][:, :], K.combine1_dram[e].broadcast_to([P, N])).then_inc(w_loaded[s], 16)

            weights(0, 1)
            weights(1, 0)
            sp.wait_ge(one_ready, 1)
            sp.dma_start(K.combine1_dram[0], one_row[:, :]).then_inc(c_stored, 16)
            sp.wait_ge(c_stored, 16)
            weighting(0, 1)
            sp.wait_ge(cT_ready, NB)
            sp.dma_start(K.combine1_dram.rearrange("e o n -> (e o) n")[1:E1, :], cT[:, :]).then_inc(c_stored, 16)
            sp.wait_ge(c_stored, 32)
            weighting(1, 0)
            sp.wait_ge(y_mm, UE)
            weights(2, 1)
            weighting(2, 1)
            with sp.Fori(1, E0 // 2) as i:
                for s in range(2):
                    sp.wait_ge(y_mm, i * (2 * UE) + s * UE)
                    weights(i * 2 + (1 + s), s)
                    weighting(i * 2 + (1 + s), s)
            sp.wait_ge(o_ready, NB)
            sp.dma_start(K.out.rearrange("(t p) d -> p t d", p=P), o[:, :].rearrange("p (t d) -> p t d", d=D)).then_inc(o_stored, 16)
            sp.wait_ge(o_stored, 16)

        def experts(eng, body):
            body(1, 0, 0)
            for s in range(2):
                body(s, 0, UE * (1 + s))
            with eng.Fori(1, E0 // 2) as i:
                for s in range(2):
                    body(s, i, i * (2 * UE) + UE * (1 + s))

        @block.tensor
        def _(pe):
            for t in range(NT):
                mm = pe.matmul(ps[:, 0, t * E0:(t + 1) * E0], xT[:, t * P:(t + 1) * P], gw[:, :], start=True, stop=True)
            mm.then_inc(logits_mm, 1)
            pe.wait_ge(router.sem, Router.STEPS)
            for t in range(NT):
                pe.transpose(ps[0:E0, t // TPB, (t % TPB) * P:(t % TPB + 1) * P], router.w[:, t * E0:(t + 1) * E0],
                             ident[:, :]).then_inc(c_turned, 1)
            pe.wait_ge(cT_ready, NB)

            def out_product(u, s, b, ft, start=False):
                pe.wait_ge(h_ready, u + 1)
                pe.matmul(ps[:, NB + b, :], w2[s][:, ft * D:(ft + 1) * D], blk(hs, b * FT1 + ft), start=start, stop=True,
                          skip_group_check=True).then_inc(y_mm, 1)

            def body(s, i, u0):
                shared = isinstance(u0, int) and u0 == 0
                second = isinstance(u0, int) and u0 == UE
                pe.wait_ge(w_loaded[s], 64 if shared else (i * 64 + (128 if s else 64)))
                for b in range(NB):
                    for ft in range(FT1):
                        ge(pe, h_mult, u0 + (b * FT1 + ft - 1))
                        pe.matmul(ps[:, ft, :], w1[s][:, ft * P:(ft + 1) * P], blk(xT, b), start=True, stop=True)
                        pe.matmul(ps[:, FT1 + ft, :], w3[s][:, ft * P:(ft + 1) * P], blk(xT, b), start=True,
                                  stop=True).then_inc(h_mm, 1)
                    if not (shared and b == 0):
                        for ft in range(FT1):
                            out_product(u0 + ((b - 1) * FT1 + ft), s if b else 1 - s, (b - 1) % NB, ft,
                                        start=(ft == 0 and (shared or (second and b == 0))))

            experts(pe, body)
            for ft in range(FT1):
                out_product(E1 * UE - FT1 + ft, 1, NB - 1, ft)
            for t in range(NT):
                pe.wait_ge(p_ready, t // TPB + 1)
                pe.transpose(ps[:, t // TPB, (t % TPB) * P:(t % TPB + 1) * P], o[:, t * P:(t + 1) * P],
                             ident[:, :]).then_inc(p_turned, 1)

        @block.scalar
        def _(act):
            router.scalar(act, Router.LOGITS)
            for b in range(NB):
                act.wait_ge(c_turned, TPB * (b + 1))
                act.activation(blk(cT, b), ps[0:E0, b, :], ACT.Copy).then_inc(cT_ready, 1)

            def body(s, i, u0):
                for b in range(NB):
                    for ft in range(FT1):
                        k = b * FT1 + ft
                        act.wait_ge(h_mm, u0 + (k + 1))
                        ge(act, h_mult, u0 + (k - SLOTS + 1))
                        act.activation(blk(hg, k), ps[:, ft, :], ACT.Silu).then_inc(h_gated, 1)

            experts(act, body)
            for b in range(NB):
                act.wait_ge(y_mm, E1 * UE - (NB - 1 - b) * FT1)
                act.activation(blk(g1, b), ps[:, NB + b, :], ACT.Silu).then_inc(g_ready, 1)

        @block.vector
        def _(dve):
            dve.memset(one_row[:, :], 1.0).then_inc(one_ready, 1)
            dve.wait_ge(logits_mm, 1)
            router.vector(dve, ps[:, 0, 0:NT * E0], None)

            def body(s, i, u0):
                for b in range(NB):
                    for ft in range(FT1):
                        k = b * FT1 + ft
                        dve.wait_ge(h_gated, u0 + (k + 1))
                        ge(dve, h_ready, u0 + (k - SLOTS + 1))
                        dve.tensor_tensor(blk(hu, k), blk(hg, k), ps[:, FT1 + ft, :], ALU.mult).then_inc(h_mult, 1)

            experts(dve, body)
            for b in range(NB):
                dve.wait_ge(g_ready, b + 1)
                dve.tensor_tensor(blk(o, b), blk(K.sT, b), blk(g1, b), ALU.mult).then_inc(p_ready, 1)
            for b in range(NB):
                dve.wait_ge(p_turned, TPB * (b + 1))
                dve.tensor_tensor(blk(o, b), ps[:, b, :], blk(K.x1, b), ALU.add).then_inc(o_ready, 1)

        @block.gpsimd
        def _(pool):
            def body(s, i, u0):
                shared = isinstance(u0, int) and u0 == 0
                pool.wait_ge(w_loaded[s], 64 if shared else (i * 64 + (128 if s else 64)))
                for b in range(NB):
                    for ft in range(FT1):
                        k = b * FT1 + ft
                        pool.wait_ge(h_mult, u0 + (k + 1))
                        ge(pool, y_mm, u0 + (k - SLOTS + 1))
                        pool.tensor_tensor(blk(hs, k), blk(hu, k), blk(cb[s], b), ALU.mult).then_inc(h_ready, 1)

            experts(pool, body)


def two_blocks_kernel(nc, t, out, stop_after=99):
    with ExitStack() as ctx:
        K = Kit()
        K.out = out
        (K.x, K.cols_dram, K.rows_dram, K.f0_wv, K.f0_wo, K.f0_gate_w, K.f0_b2, K.f0_w1, K.f0_w2, K.f0_b1,
         K.a0_wv, K.a0_bv, K.a0_wqk, K.a0_cols, K.a0_wo, K.a1_wq, K.a1_wk, K.a1_wv, K.f1_router_w, K.f1_w1,
         K.f1_w3, K.f1_w2) = (t[n] for n in NAMES)
        K.combine_dram = nc.dram_tensor("combine0", [E0, 1, N], F32, kind="Internal").ap()
        K.combine1_dram = nc.dram_tensor("combine1", [E1, 1, N], F32, kind="Internal").ap()
        sb = lambda n, w, dt=F32: ctx.enter_context(nc.sbuf_tensor(n, [P, w], dt))
        K.ps = ctx.enter_context(nc.psum_tensor("ps", [P, 8, BLK], F32))
        K.ident, K.cols, K.rows = sb("ident", P), sb("cols", NCOL), sb("rows", NROW)
        K.g0 = sb("g0", N)
        K.ident_ready = ctx.enter_context(nc.semaphore("ident_ready"))
        K.consts_loaded = ctx.enter_context(nc.semaphore("consts_loaded"))
        with ExitStack() as first:
            K.yT = first.enter_context(nc.sbuf_tensor("yT", [P, N], F32))
            with ExitStack() as a:
                K.xnT = a.enter_context(nc.sbuf_tensor("xnT", [P, N], F32))
                load_and_normalise(nc, K)
                gate_of_first_block(nc, K)
                K.values = a.enter_context(nc.sbuf_tensor("values", [P, NT * H * VW], F16))
                attention_of_first_block(nc, K)
            K.x1, K.xn1T = (first.enter_context(nc.sbuf_tensor(n, [P, N], F32)) for n in ("x1", "xn1T"))
            K.sT = K.yT
            end_of_first_block(nc, K)
            second_block(nc, K)


NAMES = ("x", "cols", "rows", "f0_wv", "f0_wo", "f0_gate_w", "f0_b2", "f0_w1", "f0_w2", "f0_b1", "a0_wv", "a0_bv",
         "a0_wqk", "a0_cols", "a0_wo", "a1_wq", "a1_wk", "a1_wv", "f1_router_w", "f1_w1", "f1_w3", "f1_w2")


def layout(i):
    import numpy as np
    i = {k: np.asarray(v) for k, v in i.items()}
    heads = lambda w: w.reshape(H, HD, D).transpose(0, 2, 1)
    twice = lambda a: np.concatenate([a, a], axis=2)
    stacked = lambda b: np.concatenate([b.reshape(H, HD)] * 2, axis=1)
    head_cols = np.stack([stacked(i["L0_attn_bq"]), stacked(i["L0_attn_bk"]),
                          np.repeat(i["L0_attn_adaptive_scale"][:, None], P, axis=1)], axis=2)
    cols = np.concatenate([np.stack([i["L0_attn_bo"], i["L0_ffn_in_proj_b"][2 * D:], i["L0_ffn_out_b"],
                                     i["L1_attn_bq"], i["L1_attn_bk"]]), i["L0_ffn_b1"].reshape(E0 * FT0, P)]).T
    rows = np.concatenate([i[n] for n in ("L0_ffn_ln1_g", "L0_ffn_ln1_b", "L0_ffn_ln2_g", "L0_ffn_ln2_b",
                                          "L0_attn_gamma", "L0_attn_beta", "L1_attn_bv", "L0_ffn_gate_b")])
    t = {
        "x": i["L0_attn_x"].reshape(N, D), "cols": cols, "rows": rows[None],
        "f0_wv": i["L0_ffn_in_proj_w"][2 * D:].T, "f0_wo": i["L0_ffn_out_w"].T, "f0_gate_w": i["L0_ffn_gate_w"].T,
        "f0_b2": i["L0_ffn_b2"], "f0_w1": i["L0_ffn_w1"].transpose(0, 2, 1),
        "f0_w2": i["L0_ffn_w2"].transpose(0, 2, 1).reshape(E0, FT0, P, D).transpose(0, 2, 1, 3).reshape(E0, P, FT0 * D),
        "f0_b1": i["L0_ffn_b1"].reshape(E0, FT0, P).transpose(0, 2, 1),
        "a0_wv": i["L0_attn_Wv"].T, "a0_bv": i["L0_attn_bv"][None],
        "a0_wqk": np.concatenate([twice(heads(i["L0_attn_Wq"])), twice(heads(i["L0_attn_Wk"]))], axis=2),
        "a0_cols": head_cols, "a0_wo": i["L0_attn_Wo"].T.reshape(H // 2, P, D),
        "a1_wq": i["L1_attn_Wq"], "a1_wk": i["L1_attn_Wk"], "a1_wv": i["L1_attn_Wv"], "f1_router_w": i["L1_ffn_w_router"],
        "f1_w1": np.concatenate([i["L1_ffn_sw1"][None], i["L1_ffn_w1"]]),
        "f1_w3": np.concatenate([i["L1_ffn_sw3"][None], i["L1_ffn_w3"]]),
        "f1_w2": np.concatenate([i["L1_ffn_sw2"][None], i["L1_ffn_w2"]]),
    }
    return {n: np.ascontiguousarray(a) for n, a in t.items()}


def kernel(**inputs):
    import concourse.bacc as _bacc
    from concourse.bass_utils import run_bass_kernel_spmd as _run

    nc = _bacc.Bacc("TRN2", target_bir_lowering=False, num_devices=1)
    arrays = {f"in_{n}": a for n, a in layout(inputs).items()}
    aps = {n: nc.dram_tensor(f"in_{n}", arrays[f"in_{n}"].shape, F32, kind="ExternalInput").ap() for n in NAMES}
    out = nc.dram_tensor("out", (N, D), F32, kind="ExternalOutput").ap()
    two_blocks_kernel(nc, aps, out)
    r = _run(nc, [arrays], core_ids=[0])
    return r.results[0]["out"].reshape(1, N, D)
```

```python
from contextlib import ExitStack

import concourse.bass as bass
from concourse import mybir

F32 = mybir.dt.float32
F32R = mybir.dt.float32r
BF16 = mybir.dt.bfloat16
F16 = mybir.dt.float16
ALU = mybir.AluOpType
ACT = mybir.ActivationFunctionType
AX_X = mybir.AxisListType.X

P = 128
N = 2048
D = 128
NT = N // P
BLK = 512
NB = N // BLK
TPB = BLK // P
H = 16
HD = 64
VW = 2 * HD + 1
E0 = 8
FT0 = 4
E1 = 9
FT1 = 2
EPS = 1e-5
BIG = 1e30

C_BO, C_VB, C_OUTB, C_Q1B, C_K1B = range(5)
C_B1 = 5
NCOL = C_B1 + E0 * FT0
ROWS = {}
_at = 0
for _n, _w in (("ln1_g", D), ("ln1_b", D), ("ln2_g", D), ("ln2_b", D), ("gamma", D), ("beta", D),
               ("v1b", D), ("gate_b", E0)):
    ROWS[_n] = (_at, _w)
    _at += _w
NROW = _at


class Count:

    def __init__(self, i, times, plus):
        self.i, self.times, self.plus = i, times, plus

    def __add__(self, c):
        return Count(self.i, self.times, self.plus + c)

    def __sub__(self, c):
        return self + -c

    def __mul__(self, c):
        return Count(self.i, self.times * c, self.plus * c)

    def value(self):
        return self.i * self.times + self.plus


BASES = {}


def base(eng, sem, value):
    key = (id(value.i), sem.name, value.times)
    if key not in BASES:
        register = eng.alloc_register(f"{sem.name}_base")
        eng.reg_mul(register, value.i, value.times)
        BASES[key] = eng.snap(register, donate=True)
    return BASES[key]


def ge(eng, sem, value):
    if isinstance(value, Count):
        value = value.value() if isinstance(value.i, int) else base(eng, sem, value) + value.plus
    if not (isinstance(value, int) and value <= 0):
        eng.wait_ge(sem, value)


def spread(ap, n):
    return ap.rearrange("p (o w) -> p o w", o=1).broadcast_to([P, n, ap.shape[1]])


def each(ap, w):
    return ap.rearrange("p (n o) -> p n o", o=1).broadcast_to([P, ap.shape[1], w])


class Norm:

    def __init__(self, ctx, nc, name):
        self.bn = ctx.enter_context(nc.semaphore(f"{name}_bn"))
        self.mv = ctx.enter_context(nc.semaphore(f"{name}_mv"))
        self.var = ctx.enter_context(nc.semaphore(f"{name}_var"))
        self.sd = ctx.enter_context(nc.semaphore(f"{name}_sd"))
        self.r = ctx.enter_context(nc.semaphore(f"{name}_rstd"))
        sb = lambda what, w: ctx.enter_context(nc.sbuf_tensor(f"{name}_{what}", [P, w], F32))
        self.st = sb("stats", NT * 6)
        self.mean_var = sb("mean_var", NT * 2)
        self.ve, self.root, self.rstd, self.t = (sb(w, NT) for w in ("ve", "root", "rstd", "t"))

    def mean(self, t):
        return self.mean_var[:, 2 * t:2 * t + 1]

    def vector(self, dve, src, ready=None):
        for t in range(NT):
            if ready:
                ready(t)
            dve.bn_stats(self.st[:, 6 * t:6 * t + 6], src[:, t * D:(t + 1) * D]).then_inc(self.bn, 1)
        for t in range(NT):
            dve.wait_ge(self.bn, t + 1)
            dve.bn_aggr(self.mean_var[:, 2 * t:2 * t + 2], self.st[:, 6 * t:6 * t + 6]).then_inc(self.mv, 1)
        dve.wait_ge(self.mv, NT)
        var = self.mean_var[:, :].rearrange("p (t c) -> p t c", c=2)[:, :, 1]
        dve.tensor_scalar(self.ve[:, :], var, EPS, None, ALU.add).then_inc(self.var, 1)
        dve.wait_ge(self.sd, 1)
        dve.reciprocal(self.rstd[:, :], self.root[:, :]).then_inc(self.r, 1)
        dve.wait_ge(self.r, 1)
        dve.tensor_tensor(self.t[:, :], self.rstd[:, :], self.rstd[:, :], ALU.mult).then_inc(self.r, 1)
        dve.wait_ge(self.r, 2)
        dve.tensor_tensor(self.t[:, :], self.t[:, :], self.ve[:, :], ALU.mult).then_inc(self.r, 1)
        dve.wait_ge(self.r, 3)
        dve.tensor_scalar(self.t[:, :], self.t[:, :], -0.5, 1.5, ALU.mult, ALU.add).then_inc(self.r, 1)
        dve.wait_ge(self.r, 4)
        dve.tensor_tensor(self.rstd[:, :], self.rstd[:, :], self.t[:, :], ALU.mult).then_inc(self.r, 1)
        dve.wait_ge(self.r, 5)

    def scalar(self, act):
        act.wait_ge(self.var, 1)
        act.activation(self.root[:, :], self.ve[:, :], ACT.Sqrt).then_inc(self.sd, 1)

    def apply(self, dve, dst, src, t, done):
        dve.tensor_scalar(dst[:, t * D:(t + 1) * D], src[:, t * D:(t + 1) * D], self.mean(t),
                          self.rstd[:, t:t + 1], ALU.subtract, ALU.mult).then_inc(done, 1)


class Router:

    def __init__(self, ctx, nc, name):
        self.sem = ctx.enter_context(nc.semaphore(f"{name}_route"))
        self.ex = ctx.enter_context(nc.semaphore(f"{name}_route_exp"))
        sb = lambda what, w: ctx.enter_context(nc.sbuf_tensor(f"{name}_{what}", [P, w], F32))
        self.lg, self.pr, self.eq, self.one, self.rest, self.two, self.w = (
            sb(x, NT * E0) for x in ("logits", "probs", "eq", "first", "rest", "second", "combine"))
        self.m = sb("top", NT)
        self.order = ctx.enter_context(nc.sbuf_tensor(f"{name}_order", [P, NT * E0], F32))
        self.n = 0

    def v(self, t):
        return t[:, :].rearrange("p (t e) -> p t e", e=E0)

    def step(self, dve, ins):
        self.n += 1
        ins.then_inc(self.sem, 1)
        dve.wait_ge(self.sem, self.n)

    def vector(self, dve, logits_psum, bias):
        v, m = self.v, self.m
        for e in range(E0):
            self.step(dve, dve.memset(v(self.order)[:, :, e], float(E0 - e)))
        if bias is None:
            self.step(dve, dve.tensor_copy(self.lg[:, :], logits_psum))
        else:
            self.step(dve, dve.tensor_tensor(v(self.lg), logits_psum.rearrange("p (t e) -> p t e", e=E0),
                                             spread(bias, NT), ALU.add))
        self.step(dve, dve.tensor_reduce(m[:, :], v(self.lg), AX_X, ALU.max))
        self.step(dve, dve.tensor_tensor(v(self.lg), v(self.lg), each(m[:, :], E0), ALU.subtract))
        dve.wait_ge(self.ex, 1)
        self.step(dve, dve.tensor_reduce(m[:, :], v(self.pr), AX_X, ALU.add))
        self.step(dve, dve.reciprocal(m[:, :], m[:, :]))
        self.step(dve, dve.tensor_tensor(v(self.pr), v(self.pr), each(m[:, :], E0), ALU.mult))
        self.pick(dve, self.pr, self.one)
        self.step(dve, dve.tensor_tensor(self.rest[:, :], self.pr[:, :], self.one[:, :], ALU.subtract))
        self.step(dve, dve.tensor_tensor(self.rest[:, :], self.rest[:, :], self.one[:, :], ALU.subtract))
        self.pick(dve, self.rest, self.two)
        self.step(dve, dve.tensor_tensor(self.one[:, :], self.one[:, :], self.two[:, :], ALU.add))
        self.step(dve, dve.tensor_tensor(self.w[:, :], self.pr[:, :], self.one[:, :], ALU.mult))
        self.step(dve, dve.tensor_reduce(m[:, :], v(self.w), AX_X, ALU.add))
        self.step(dve, dve.reciprocal(m[:, :], m[:, :]))
        self.step(dve, dve.tensor_tensor(v(self.w), v(self.w), each(m[:, :], E0), ALU.mult))
        assert self.n == self.STEPS

    def pick(self, dve, values, out):
        v, m = self.v, self.m
        self.step(dve, dve.tensor_reduce(m[:, :], v(values), AX_X, ALU.max))
        self.step(dve, dve.tensor_tensor(v(self.eq), v(values), each(m[:, :], E0), ALU.is_ge))
        self.step(dve, dve.tensor_tensor(self.eq[:, :], self.eq[:, :], self.order[:, :], ALU.mult))
        self.step(dve, dve.tensor_reduce(m[:, :], v(self.eq), AX_X, ALU.max))
        self.step(dve, dve.tensor_tensor(v(out), v(self.eq), each(m[:, :], E0), ALU.is_ge))

    def scalar(self, act, logits_steps):
        act.wait_ge(self.sem, logits_steps)
        act.activation(self.pr[:, :], self.lg[:, :], ACT.Exp).then_inc(self.ex, 1)

    LOGITS = E0 + 3
    STEPS = LOGITS + 3 + 5 + 2 + 5 + 5


def load_and_normalise(nc, K):
    ps, ident, xnT = K.ps, K.ident, K.xnT
    with ExitStack() as ctx:
        x = ctx.enter_context(nc.sbuf_tensor("x_in", [P, N], F32))
        xn = ctx.enter_context(nc.sbuf_tensor("xn_tok", [P, N], F32))
        norm = Norm(ctx, nc, "n_in")
        sem = lambda n: ctx.enter_context(nc.semaphore(n))
        x_loaded = [sem(f"x_loaded{b}") for b in range(NB)]
        zeroed, xn_ready, xn_turned, xnT_ready = sem("ident_zeroed"), sem("xn_ready"), sem("xn_turned"), sem("xnT_ready")
        block = ctx.enter_context(nc.Block())

        @block.sync
        def _(sp):
            for b in range(NB):
                sp.dma_start(x[:, b * BLK:(b + 1) * BLK].rearrange("p (t d) -> p t d", d=D),
                             K.x[b * BLK:(b + 1) * BLK, :].rearrange("(t p) d -> p t d", p=P)).then_inc(x_loaded[b], 16)
            sp.dma_start(K.cols[:, :], K.cols_dram).then_inc(K.consts_loaded, 16)
            sp.dma_start(K.rows[:, :], K.rows_dram.broadcast_to([P, NROW])).then_inc(K.consts_loaded, 16)

        @block.gpsimd
        def _(pool):
            pool.memset(ident[:, :], 0.0).then_inc(zeroed, 1)
            pool.wait_ge(zeroed, 1)
            pool.affine_select(out=ident[:, :], in_=ident[:, :], compare_op=ALU.not_equal, fill=1.0,
                               base=0, pattern=[[-1, P]], channel_multiplier=1).then_inc(K.ident_ready, 1)

        @block.vector
        def _(dve):
            norm.vector(dve, x, lambda t: dve.wait_ge(x_loaded[t // TPB], 16))
            for t in range(NT):
                norm.apply(dve, xn, x, t, xn_ready)

        @block.tensor
        def _(pe):
            pe.wait_ge(K.ident_ready, 1)
            for t in range(NT):
                pe.wait_ge(xn_ready, t + 1)
                pe.transpose(ps[:, t // TPB, (t % TPB) * P:(t % TPB + 1) * P], xn[:, t * D:(t + 1) * D],
                             ident[:, :]).then_inc(xn_turned, 1)

        @block.scalar
        def _(act):
            norm.scalar(act)
            for b in range(NB):
                act.wait_ge(xn_turned, TPB * (b + 1))
                act.activation(xnT[:, b * BLK:(b + 1) * BLK], ps[:, b, :], ACT.Copy).then_inc(xnT_ready, 1)


def blk(t, b):
    return t[:, b * BLK:(b + 1) * BLK]


def gate_of_first_block(nc, K):
    ps, ident, xnT = K.ps, K.ident, K.xnT
    with ExitStack() as ctx:
        sb = lambda n, w: ctx.enter_context(nc.sbuf_tensor(n, [P, w], F32))
        sem = lambda n: ctx.enter_context(nc.semaphore(n))
        wv, wo, gw = sb("f0_wv", D), sb("f0_wo", D), sb("f0_gate_w", E0)
        b2 = ctx.enter_context(nc.sbuf_tensor("f0_b2", [E0, D], F32))
        cT = ctx.enter_context(nc.sbuf_tensor("f0_combineT", [E0, N], F32))
        vT, r1T, r1, x1, x1T, r2T, r2 = (sb(f"f0_{n}", N) for n in ("vT", "r1T", "r1", "x1", "x1T", "r2T", "r2"))
        w1 = [sb(f"f0_w1_{h}", FT0 * P) for h in range(2)]
        w2 = [sb(f"f0_w2_{h}", FT0 * D) for h in range(2)]
        b1 = [sb(f"f0_b1_{h}", FT0) for h in range(2)]
        cb = [sb(f"f0_weight_{h}", N) for h in range(2)]
        hr = sb("f0_hidden", 8 * BLK)
        hs = sb("f0_hidden_weighted", 8 * BLK)
        norm1, norm2, router = Norm(ctx, nc, "f0_n1"), Norm(ctx, nc, "f0_n2"), Router(ctx, nc, "f0")
        loaded = sem("f0_loaded")
        w_loaded = [sem(f"f0_w_loaded{h}") for h in range(2)]
        v_mm, v_ready, o_mm, r1T_ready = sem("f0_v_mm"), sem("f0_v_ready"), sem("f0_o_mm"), sem("f0_r1T_ready")
        r1_turned, r1_ready, x1_step, x1_ready = sem("f0_r1_turned"), sem("f0_r1_ready"), sem("f0_x1_step"), sem("f0_x1_ready")
        x1_turned, x1T_ready, logits_mm, routed = sem("f0_x1_turned"), sem("f0_x1T_ready"), sem("f0_logits_mm"), sem("f0_routed")
        c_turned, cT_ready, c_stored = sem("f0_c_turned"), sem("f0_cT_ready"), sem("f0_c_stored")
        h_mm, h_relu, h_weighted, y_mm = sem("f0_h_mm"), sem("f0_h_relu"), sem("f0_h_weighted"), sem("f0_y_mm")
        r2T_ready, r2_turned, r2_ready, x2_step, x2_ready, g_ready = (
            sem(f"f0_{n}") for n in ("r2T_ready", "r2_turned", "r2_ready", "x2_step", "x2_ready", "g_ready"))
        UE = NB * FT0
        block = ctx.enter_context(nc.Block())

        @block.sync
        def _(sp):
            sp.dma_start(wv[:, :], K.f0_wv).then_inc(loaded, 16)
            sp.dma_start(wo[:, :], K.f0_wo).then_inc(loaded, 16)
            sp.dma_start(gw[:, :], K.f0_gate_w).then_inc(loaded, 16)
            sp.dma_start(b2[:, :], K.f0_b2).then_inc(loaded, 16)

            def weights(e, half):
                sp.dma_start(w1[half][:, :], K.f0_w1[e]).then_inc(w_loaded[half], 16)
                sp.dma_start(w2[half][:, :], K.f0_w2[e]).then_inc(w_loaded[half], 16)
                sp.dma_start(b1[half][:, :], K.f0_b1[e]).then_inc(w_loaded[half], 16)

            def weighting(e, half):
                sp.dma_start(cb[half][:, :], K.combine_dram[e].broadcast_to([P, N])).then_inc(w_loaded[half], 16)

            for half in range(2):
                weights(half, half)
            sp.wait_ge(cT_ready, NB)
            sp.dma_start(K.combine_dram.rearrange("e o n -> (e o) n")[0:E0, :], cT[:, :]).then_inc(c_stored, 16)
            sp.wait_ge(c_stored, 16)
            for half in range(2):
                weighting(half, half)
            with sp.Fori(1, E0 // 2) as i:
                for half in range(2):
                    sp.wait_ge(y_mm, i * (2 * UE) + (half - 1) * UE)
                    weights(i * 2 + half, half)
                    weighting(i * 2 + half, half)

        @block.tensor
        def _(pe):
            pe.wait_ge(loaded, 64)
            for b in range(NB):
                pe.matmul(ps[:, b, :], wv[:, :], blk(xnT, b), start=True, stop=True).then_inc(v_mm, 1)
            for b in range(NB):
                pe.wait_ge(v_ready, b + 1)
                pe.matmul(ps[:, NB + b, :], wo[:, :], blk(vT, b), start=True, stop=True).then_inc(o_mm, 1)

            def turn(src, t, base, done):
                pe.transpose(ps[:, base + t // TPB, (t % TPB) * P:(t % TPB + 1) * P], src[:, t * P:(t + 1) * P],
                             ident[:, :]).then_inc(done, 1)

            for t in range(NT):
                pe.wait_ge(r1T_ready, t // TPB + 1)
                turn(r1T, t, 0, r1_turned)
            for t in range(NT):
                pe.wait_ge(x1_ready, t // TPB + 1)
                turn(x1, t, NB, x1_turned)
            for t in range(NT):
                pe.wait_ge(x1T_ready, t // TPB + 1)
                mm = pe.matmul(ps[:, 0, t * E0:(t + 1) * E0], x1T[:, t * P:(t + 1) * P], gw[:, :], start=True, stop=True)
            mm.then_inc(logits_mm, 1)
            pe.wait_ge(router.sem, Router.STEPS)
            for t in range(NT):
                pe.transpose(ps[0:E0, t // TPB, (t % TPB) * P:(t % TPB + 1) * P], router.w[:, t * E0:(t + 1) * E0],
                             ident[:, :]).then_inc(c_turned, 1)
            for b in range(NB):
                pe.wait_ge(cT_ready, b + 1)
                pe.matmul(ps[:, NB + b, :], b2[:, :], blk(cT, b), start=True, stop=True, skip_group_check=True)

            def out_product(u, half, b, ft):
                pe.wait_ge(h_weighted, u + 1)
                s = (b % 2) * FT0 + ft
                pe.matmul(ps[:, NB + b, :], w2[half][:, ft * D:(ft + 1) * D], blk(hs, s), start=False, stop=True,
                          skip_group_check=True).then_inc(y_mm, 1)

            def pair(i, first=False):
                base = i * (2 * UE)
                for half in range(2):
                    pe.wait_ge(w_loaded[half], i * 64 + 64)
                    for b in range(NB):
                        u0 = half * UE + b * FT0
                        for ft in range(FT0):
                            ge(pe, h_relu, base + (u0 + ft - FT0 + 1))
                            pe.matmul(ps[:, ft, :], w1[half][:, ft * P:(ft + 1) * P], blk(x1T, b),
                                      start=True, stop=True).then_inc(h_mm, 1)
                        if not (first and u0 == 0):
                            for ft in range(FT0):
                                out_product(base + (u0 - FT0 + ft), half if b else 1 - half, (b - 1) % NB, ft)

            pair(0, True)
            with pe.Fori(1, E0 // 2) as i:
                pair(i)
            for ft in range(FT0):
                out_product(E0 * UE - FT0 + ft, 1, NB - 1, ft)
            for t in range(NT):
                pe.wait_ge(r2T_ready, t // TPB + 1)
                turn(r2T, t, 0, r2_turned)

        @block.scalar
        def _(act):
            def copy_out(dst, done, ready, base, w=P):
                for b in range(NB):
                    act.wait_ge(ready, TPB * (b + 1))
                    act.activation(blk(dst, b), ps[0:w, base + b, :], ACT.Copy).then_inc(done, 1)

            act.wait_ge(K.consts_loaded, 32)
            for b in range(NB):
                act.wait_ge(v_mm, b + 1)
                act.activation(blk(vT, b), ps[:, b, :], ACT.Identity, bias=K.col(C_VB)).then_inc(v_ready, 1)
            copy_out(r1, r1_ready, r1_turned, 0)
            norm1.scalar(act)
            copy_out(x1T, x1T_ready, x1_turned, NB)
            router.scalar(act, Router.LOGITS)
            copy_out(cT, cT_ready, c_turned, 0, E0)

            def pair(i):
                base = i * (2 * UE)
                for half in range(2):
                    for b in range(NB):
                        for ft in range(FT0):
                            u = half * UE + b * FT0 + ft
                            act.wait_ge(h_mm, base + (u + 1))
                            ge(act, h_weighted, base + (u - 7))
                            act.activation(blk(hr, u % 8), ps[:, ft, :], ACT.Relu,
                                           bias=b1[half][:, ft:ft + 1]).then_inc(h_relu, 1)

            pair(0)
            with act.Fori(1, E0 // 2) as i:
                pair(i)
            copy_out(r2, r2_ready, r2_turned, 0)
            norm2.scalar(act)
            for b in range(NB):
                act.wait_ge(x2_ready, b + 1)
                act.activation(blk(K.g0, b), blk(r2T, b), ACT.Silu).then_inc(g_ready, 1)

        @block.vector
        def _(dve):
            dve.wait_ge(K.consts_loaded, 32)
            for b in range(NB):
                dve.wait_ge(o_mm, b + 1)
                dve.scalar_tensor_tensor(out=blk(r1T, b), in0=ps[:, NB + b, :], scalar=K.col(C_OUTB),
                                         in1=blk(xnT, b), op0=ALU.add, op1=ALU.add).then_inc(r1T_ready, 1)
            affine_norm(dve, K, norm1, r1, x1, r1_ready, x1_step, x1_ready, "ln1_g", "ln1_b")
            dve.wait_ge(logits_mm, 1)
            router.vector(dve, ps[:, 0, 0:NT * E0], K.row("gate_b"))

            def pair(i):
                base = i * (2 * UE)
                for half in range(2):
                    dve.wait_ge(w_loaded[half], i * 64 + 64)
                    for b in range(NB):
                        for ft in range(FT0):
                            u = half * UE + b * FT0 + ft
                            dve.wait_ge(h_relu, base + (u + 1))
                            ge(dve, y_mm, base + (u - 7))
                            dve.tensor_tensor(blk(hs, u % 8), blk(hr, u % 8), blk(cb[half], b),
                                              ALU.mult).then_inc(h_weighted, 1)

            pair(0)
            with dve.Fori(1, E0 // 2) as i:
                pair(i)
            dve.wait_ge(y_mm, E0 * UE)
            for b in range(NB):
                dve.tensor_tensor(blk(r2T, b), ps[:, NB + b, :], blk(x1T, b), ALU.add).then_inc(r2T_ready, 1)
            affine_norm(dve, K, norm2, r2, r2T, r2_ready, x2_step, x2_ready, "ln2_g", "ln2_b")


def affine_norm(dve, K, norm, src, dst, src_ready, step, done, g, b, count=0):
    norm.vector(dve, src, lambda t: dve.wait_ge(src_ready, t // TPB + 1))
    n = count
    for k in range(NB):
        for t in range(k * TPB, (k + 1) * TPB):
            norm.apply(dve, dst, src, t, step)
        n += TPB
        tiles = blk(dst, k).rearrange("p (t d) -> p t d", d=D)
        dve.wait_ge(step, n)
        dve.tensor_tensor(tiles, tiles, spread(K.row(g), TPB), ALU.mult).then_inc(step, 1)
        n += 1
        dve.wait_ge(step, n)
        dve.tensor_tensor(tiles, tiles, spread(K.row(b), TPB), ALU.add).then_inc(done, 1)


class Kit:

    def col(self, c):
        return self.cols[:, c:c + 1]

    def row(self, name):
        at, w = ROWS[name]
        return self.rows[:, at:at + w]


STEPS = NB * NT
LAG = 3
SB = 3
PBUF = 5
O_BANK = 3
OW = HD + 1
GROUP = 2
M_BANK = 5
W_BANK = 7
MU = NT * NB
ON_VECTOR = (2, 6, 10, 14)
NV = len(ON_VECTOR)
PROJ_AT = {0: 0, 1: 1, 2: 2, 3: 3}
LAST_W = 8
ROWS_AT = {43: ("N", 0), 63: ("N", 1)}
TOPS_AT = {41: 0, 62: 1}
TURN = ({6: ("T", 3), 8: ("W", 3)},
        {21: ("T", 0), 36: ("W", 0), 39: ("T", 1), 52: ("W", 1), 55: ("T", 2), 60: ("W", 2)})
MAX_FROM, MAX_TO = 8, 62
MAX_TWICE = (12, 16, 20, 24, 28, 32, 40, 44, 48, 56)
assert MAX_TO - MAX_FROM + len(MAX_TWICE) == MU


def max_units(k):
    done = lambda j: max(0, min(j, MAX_TO) - MAX_FROM) + sum(e < j for e in MAX_TWICE)
    return range(done(k), done(k + 1))


VALUE_UNITS = NT * 2
VALUES_AT = {2 * u: u for u in range(VALUE_UNITS)}


def max_tile(u):
    half, rest = divmod(u, MU // 2)
    mb, nt = divmod(rest, NT // 2)
    return half * (NT // 2) + nt, mb


def before(k, n):
    return k - n + 1 if k >= n else next(j + 1 for j in range(-1, -STEPS, -1) if (j + STEPS) % n == k)


def lower_on_vector(mt):
    return mt in ON_VECTOR


def lower_count(k, on_vector):
    full, part = divmod(k, NT)
    n = sum(lower_on_vector(m) == on_vector for m in range(part))
    return full * (NV if on_vector else NT - NV) + n


def attention_of_first_block(nc, K):
    ps, ident, xnT, yT = K.ps, K.ident, K.xnT, K.yT
    bank = lambda b: ps[:, b, :]
    values = K.values[:, :].rearrange("p (t h w) -> p t h w", t=NT, h=H)
    with ExitStack() as ctx:
        sb = lambda n, w, dt=F32, p=P: ctx.enter_context(nc.sbuf_tensor(n, [p, w], dt))
        sem = lambda n: ctx.enter_context(nc.semaphore(n))
        two = lambda n, w, dt=F32: [sb(f"{n}{s}", w, dt) for s in range(2)]
        q_stack, k_stack = two("q_stack", N, F32R), two("k_stack", N, F32R)
        q_row, k_low = two("q_row", N, F32R), two("k_low", N, F32R)
        v_head = two("v_head", NT * VW, F16)
        w_kq = two("w_kq", P)
        head_cols = two("head_cols", 2)
        kq_cols = two("kq_cols", 2)
        zeros = ctx.enter_context(nc.sbuf_tensor("zeros", [NT, P], F32))
        wo = sb("a0_wo", D)
        kq32 = two("kq32_", BLK)
        maxima, top = sb("maxima", MU), sb("top", NT)
        row = ctx.enter_context(nc.sbuf_tensor("minus_max", [NT // 2, 2 * P], F32R))
        prob, prob_low = sb("prob", PBUF * BLK), sb("prob_low", PBUF * BLK, F16)
        o_rz = two("o_rz", TPB)
        ctxt = sb("contexts", NT * P)
        ctxT = sb("contextsT", BLK)
        prob_high = prob[:, :].bitcast(BF16).rearrange("p (n two) -> p n two", two=2)[:, :, 1]
        O = ps[:, O_BANK:O_BANK + 2, 0:TPB * OW].rearrange("p b (j w) -> p b j w", w=OW)

        wv, v_bias, all_ones = ctxt[:, 0:H * HD], q_row[1][:, H * HD:2 * H * HD], q_row[1][:, 0:P]
        v_bias_low, v32 = k_stack[1][0:1, 0:H * HD], prob
        bv = ctxt[0:1, H * HD:2 * H * HD]
        v_loaded, v_bias_step, v_bias_ready = (sem(f"v_{n}") for n in ("loaded", "bias_step", "bias_ready"))
        v_mm, v_high, v_low, y_started = (sem(n) for n in ("v_mm", "v_high", "v_low", "y_started"))
        constants_set = sem("constants_set")
        V_BIAS_SET, ZEROS_SET, K_ONES_SET, V_ONES_SET = 2, 3, 5, 6
        w_loaded = [sem(f"qk_w_loaded{s}") for s in range(2)]
        wo_loaded = sem("wo_loaded")
        row_sent = [sem(f"row_sent{n}") for n in range(2)]
        cols_step = sem("kq_cols_step")
        row_cleared, low_moved, high_moved = (sem(n) for n in ("row_cleared", "low_moved", "high_moved"))
        q_moved, k_doubled = ([sem(f"{n}{b}") for b in range(NB)] for n in ("q_moved", "k_doubled"))
        proj_ready, proj_done = sem("proj_ready"), sem("proj_done")
        job_ready, job_done = sem("job_ready"), sem("job_done")
        rounded, split = sem("kq_rounded"), sem("kq_split")
        max_mm, max_taken, top_ready = sem("max_mm"), sem("max_taken"), sem("top_ready")
        v_moved = sem("v_moved")
        scored, exp_done, low_pool, low_vector, pv_done = (
            sem(n) for n in ("scored", "exp_done", "low_pool", "low_vector", "pv_done"))
        o_rz_ready, ctx_ready = sem("o_rz_ready"), sem("ctx_ready")
        block = ctx.enter_context(nc.Block())

        class Half:

            def __init__(self, i, s, main=True, prep=True):
                self.i, self.s, self.main, self.prep = i, s, main, prep
                self.pair = Count(i, 1, 0)
                self.h = Count(i, 2, s) if main else Count(0, 0, -1)
                self.g = self.h + 1
                jobs = {}
                if prep:
                    jobs |= ROWS_AT
                if main:
                    jobs |= TURN[s]
                if main and isinstance(i, int) and i == 0 and s == 0:
                    jobs = {k: j for k, j in jobs.items() if k not in TURN[0]}
                self.jobs = dict(sorted(jobs.items()))
                before = sorted(self.jobs)
                self.index = {k: n for n, k in enumerate(before)}
                self.weights = Count(i, 1, s) if main else Count(0, 0, 0)
                self.start = isinstance(i, int) and i == 0 and s == 0
                self.end = isinstance(i, int) and i == H // 2 - 1
                if not main:
                    self.job0 = Count(0, 0, 0)
                elif isinstance(i, int) and i == 0:
                    self.job0 = Count(0, 0, 2 if s == 0 else 4)
                else:
                    self.job0 = Count(i, 12, 0 if s == 0 else 4)

            def job(self, k):
                return self.job0 + self.index[k]

        def run(eng, body):
            body(Half(0, 1, main=False))
            for s in range(2):
                body(Half(0, s))
            with eng.Fori(1, H // 2 - 1) as i:
                BASES.clear()
                for s in range(2):
                    body(Half(i, s))
            BASES.clear()
            body(Half(H // 2 - 1, 0))
            body(Half(H // 2 - 1, 1, prep=False))

        def lower(eng, x, k, done):
            ge(eng, exp_done, x.h * STEPS + (k + 1))
            ge(eng, pv_done, x.h * STEPS + before(k, PBUF))
            eng.tensor_tensor(blk(prob_low, k % PBUF), blk(prob, k % PBUF), blk(prob_high, k % PBUF),
                              ALU.subtract).then_inc(done, 1)

        def value(u, first):
            t, half = divmod(u, 2)
            return values[:, t, half * 8:half * 8 + 8, first:first + HD]

        def by_head(a):
            return a.rearrange("p (h d) -> p h d", d=HD)

        def tail():
            x = Half(H // 2, 0, prep=False)
            x.job0 = Count(0, 0, (H // 2 - 1) * 12 + 10)
            return x

        @block.sync
        def _(sp):
            def load(h, s):
                sp.dma_start(w_kq[s][:, :], K.a0_wkq[h.value()]).then_inc(w_loaded[s], 16)
                sp.dma_start(head_cols[s][:, :], K.a0_cols[h.value()]).then_inc(w_loaded[s], 16)

            def load_wo(i):
                sp.dma_start(wo[:, :], K.a0_wo[i.value()]).then_inc(wo_loaded, 16)

            def move(dst, src, done):
                f32 = lambda a: a.bitcast(F32) if a.dtype == F32R else a
                sp.dma_start(f32(dst), f32(src)).then_inc(done, 16)

            sp.dma_start(bv, K.a0_bv).then_inc(v_loaded, 16)
            load(Count(0, 0, 0), 0)
            sp.dma_start(wv, K.a0_wv).then_inc(v_loaded, 16)
            load(Count(0, 0, 1), 1)
            load_wo(Count(0, 0, 0))
            sp.wait_ge(v_bias_step, 2)
            move(v_bias[1:2, :], v_bias_low, v_bias_ready)
            sp.wait_ge(constants_set, ZEROS_SET)

            def body(x):
                nxt = 1 - x.s
                if x.prep:
                    if x.main:
                        ge(sp, scored, x.h * STEPS)
                    move(q_row[nxt][HD:HD + 1, :], zeros[:, :], row_cleared)
                    for n in range(NB + 1):
                        if n < NB:
                            ge(sp, rounded, x.g * NB + (n + 1))
                            move(blk(q_row[nxt], n)[0:HD, :], blk(k_stack[nxt], n)[HD:P, :], q_moved[n])
                        if n == NB:
                            ge(sp, split, x.g * NB + NB)
                            move(k_low[nxt][0:HD, :], q_stack[nxt][0:HD, :], low_moved)
                        if n > 0:
                            ge(sp, q_moved[n - 1], x.g * 16 + 16)
                            move(blk(k_stack[nxt], n - 1)[HD:P, :], blk(k_stack[nxt], n - 1)[0:HD, :], k_doubled[n - 1])
                    ge(sp, low_moved, x.g * 16 + 16)
                    move(q_stack[nxt][0:HD, :], q_row[nxt][0:HD, :], high_moved)
                if x.main and not x.end:
                    ge(sp, split, x.h * NB + NB)
                    load(x.h + 2, x.s)
                if x.main and x.s == 0 and not x.start:
                    ge(sp, job_ready, x.job(LAST_W) + 1)
                    load_wo(x.pair)
                if x.prep:
                    for k, (_, n) in ROWS_AT.items():
                        ge(sp, job_done, x.job(k) + 1)
                        move(q_row[nxt][HD:HD + 1, n * 2 * BLK:(n + 1) * 2 * BLK], row[:, n * P:(n + 1) * P], row_sent[n])

            run(sp, body)

        @block.tensor
        def _(pe):
            def pv(x, k):
                own = k >= 0
                h, s, k = (x.h, x.s, k) if own else (x.h - 1, 1 - x.s, k + STEPS)
                nb, mt = divmod(k, NT)
                if lower_on_vector(mt):
                    ge(pe, low_vector, h * (NB * NV) + lower_count(k + 1, True))
                else:
                    ge(pe, low_pool, h * (NB * (NT - NV)) + lower_count(k + 1, False))
                if mt == 0:
                    ge(pe, ctx_ready, h * NB + (nb - 1))
                    if nb == 0:
                        ge(pe, v_moved, h + 1)
                at = k % PBUF * BLK
                buf = lambda t, j: t[:, at + j * P:at + (j + 1) * P]
                v = v_head[s][:, mt * VW:(mt + 1) * VW]
                for j in range(TPB):
                    o = O[:, nb % 2, j, :]
                    pe.matmul(o, buf(prob_high, j), v[:, 0:OW], start=(mt == 0 and j == 0), stop=False,
                              skip_group_check=True)
                    pe.matmul(o[:, 0:HD], buf(prob_high, j), v[:, OW:VW], start=False, stop=False, skip_group_check=True)
                    mm = pe.matmul(o, buf(prob_low, j), v[:, 0:OW], start=False, stop=(mt == NT - 1),
                                   skip_group_check=True)
                mm.then_inc(pv_done, 1)

            def job(x, k):
                kind, n = x.jobs[k]
                ge(pe, job_done, x.job(k))
                nxt = 1 - x.s
                if kind == "N":
                    ge(pe, top_ready, x.g * 2 + (n + 1))
                    pe.transpose(ps[0:NT // 2, W_BANK, 0:P], top[:, n * 8:(n + 1) * 8], ident[:, :]).then_inc(job_ready, 1)
                elif kind == "T":
                    ge(pe, ctx_ready, x.h * NB + (n + 1 if x.s else 0))
                    for j in range(TPB):
                        mm = pe.transpose(ps[:, W_BANK, j * P:(j + 1) * P],
                                          ctxt[:, (n * TPB + j) * P:(n * TPB + j + 1) * P], ident[:, :])
                    mm.then_inc(job_ready, 1)
                else:
                    ge(pe, wo_loaded, x.pair * 16 + 16 * x.s)
                    pe.matmul(bank(W_BANK), wo[:, :], ctxT[:, :], start=True, stop=True).then_inc(job_ready, 1)

            def unit_of_values(u):
                t, half = divmod(u, 2)
                if u == 0:
                    pe.wait_ge(v_loaded, 32)
                    pe.wait_ge(v_bias_step, 1)
                    pe.wait_ge(v_bias_ready, 16)
                ge(pe, v_high, u - SB + 1)
                pe.matmul(bank(u % SB), xnT[:, t * P:(t + 1) * P], blk(wv, half), start=True, stop=False)
                pe.matmul(bank(u % SB), all_ones, blk(v_bias, half), start=False, stop=True).then_inc(v_mm, 1)

            def scores(x, k):
                cur = x.s
                nb, mt = divmod(k, NT)
                if k == 0 and x.start:
                    pe.wait_ge(v_high, VALUE_UNITS)
                if k == 0:
                    ge(pe, low_moved, x.h * 16 + 16)
                    ge(pe, high_moved, x.h * 16 + 16)
                if k % (2 * NT) == 0:
                    ge(pe, row_sent[nb // 2], x.h * 16 + 16)
                ge(pe, exp_done, x.h * STEPS + before(k, SB))
                m = slice(mt * P, (mt + 1) * P)
                pe.matmul(bank(k % SB), k_stack[cur][:, m], blk(q_stack[cur], nb), start=True, stop=False)
                pe.matmul(bank(k % SB), k_low[cur][0:HD + 1, m], blk(q_row[cur], nb)[0:HD + 1, :], start=False,
                          stop=True).then_inc(scored, 1)

            def projection(x, n):
                nxt = 1 - x.s
                if n == 0:
                    ge(pe, w_loaded[nxt], x.weights * 32 + 32)
                if n < 2:
                    ge(pe, max_taken, x.g * MU + (n - 1))
                ge(pe, proj_done, x.g * NB + (n - 1))
                pe.matmul(bank(M_BANK + n % 2), w_kq[nxt][:, :], blk(xnT, n), start=True, stop=True).then_inc(proj_ready, 1)

            def maximum(x, u):
                nxt = 1 - x.s
                nt, mb = max_tile(u)
                if u == 0:
                    ge(pe, row_cleared, x.g * 16 + 16)
                if u < 2:
                    ge(pe, proj_done, x.g * NB + (NB - 1 + u))
                if mb == 0 and nt % TPB == 0:
                    ge(pe, q_moved[nt // TPB], x.g * 16 + 16)
                if nt == 0:
                    ge(pe, k_doubled[mb], x.g * 16 + 16)
                ge(pe, max_taken, x.g * MU + (u - 1))
                pe.matmul(bank(M_BANK + u % 2), q_row[nxt][0:HD + 1, nt * P:(nt + 1) * P],
                          blk(k_stack[nxt], mb)[0:HD + 1, :], start=True, stop=True).then_inc(max_mm, 1)

            def body(x):
                for first in range(0, STEPS, GROUP):
                    steps = range(first, first + GROUP)
                    for k in steps:
                        units = list(max_units(k)) if x.prep else []
                        if len(units) > 1:
                            maximum(x, units.pop(0))
                        if x.main:
                            scores(x, k)
                        if k in x.jobs:
                            job(x, k)
                        if x.prep and k in PROJ_AT:
                            projection(x, PROJ_AT[k])
                        if not x.main and k in VALUES_AT:
                            unit_of_values(VALUES_AT[k])
                        for u in units:
                            maximum(x, u)
                    if x.main:
                        for k in steps:
                            if not (k < LAG and x.start):
                                pv(x, k - LAG)
                if x.main and not x.prep:
                    for k in range(STEPS, STEPS + LAG):
                        pv(x, k - LAG)

            pe.wait_ge(constants_set, K_ONES_SET)
            run(pe, body)
            for k in TURN[0]:
                job(tail(), k)

        @block.scalar
        def _(act):
            def job(x, k):
                kind, n = x.jobs[k]
                if kind == "W":
                    return
                ge(act, job_ready, x.job(k) + 1)
                nxt = 1 - x.s
                if kind == "N":
                    ge(act, row_sent[n], x.g * 16)
                    act.activation(row[:, n * P:(n + 1) * P], ps[0:NT // 2, W_BANK, 0:P], ACT.Copy,
                                   scale=-1.0).then_inc(job_done, 1)
                else:
                    act.activation(ctxT[:, :], bank(W_BANK), ACT.Copy).then_inc(job_done, 1)

            def projection(x, n):
                nxt = 1 - x.s
                ge(act, proj_ready, x.g * NB + (n + 1))
                ge(act, cols_step, x.g * 2 + 2)
                ge(act, split, x.g * NB + (n - 1))
                act.activation(kq32[n % 2][:, :], bank(M_BANK + n % 2), ACT.Identity, bias=kq_cols[nxt][:, 1:2],
                               scale=kq_cols[nxt][:, 0:1]).then_inc(proj_done, 1)

            def body(x):
                for k in range(STEPS):
                    if x.main:
                        ge(act, scored, x.h * STEPS + (k + 1))
                        ge(act, pv_done, x.h * STEPS + before(k, PBUF))
                        act.activation(blk(prob, k % PBUF), bank(k % SB), ACT.Exp).then_inc(exp_done, 1)
                    if k in x.jobs:
                        job(x, k)
                    if x.prep and k in PROJ_AT:
                        projection(x, PROJ_AT[k])
                    if not x.main and k in VALUES_AT:
                        u = VALUES_AT[k]
                        act.wait_ge(v_mm, u + 1)
                        ge(act, v_low, u - PBUF + 1)
                        act.activation(blk(v32, u % PBUF), bank(u % SB), ACT.Copy)
                        act.activation(value(u, 0), by_head(bank(u % SB)), ACT.Copy).then_inc(v_high, 1)
                if not x.main:
                    act.wait_ge(v_low, VALUE_UNITS)

            run(act, body)
            for k in TURN[0]:
                job(tail(), k)

        @block.gpsimd
        def _(pool):
            pool.memset(all_ones.bitcast(F32), 1.0).then_inc(constants_set, 1)
            pool.memset(v_bias.bitcast(F32), 0.0).then_inc(constants_set, 1)
            pool.wait_ge(constants_set, V_BIAS_SET)
            pool.memset(zeros[:, :], 0.0).then_inc(constants_set, 1)
            pool.wait_ge(constants_set, ZEROS_SET)
            for s in range(2):
                pool.memset(k_low[s][HD:HD + 1, :].bitcast(F32), 1.0).then_inc(constants_set, 1)

            pool.wait_ge(constants_set, K_ONES_SET)
            pool.memset(values[:, :, :, HD], 1.0).then_inc(constants_set, 1)

            def body(x):
                if not x.main:
                    for u in range(VALUE_UNITS):
                        pool.wait_ge(v_high, u + 1)
                        pool.tensor_tensor(value(u, HD + 1), by_head(blk(v32, u % PBUF)), value(u, 0),
                                           ALU.subtract).then_inc(v_low, 1)
                if x.main:
                    for k in range(STEPS):
                        if not lower_on_vector(k % NT):
                            lower(pool, x, k, low_pool)

            run(pool, body)

        @block.vector
        def _(dve):
            def contexts(h, s, nb):
                ge(dve, pv_done, h * STEPS + (nb + 1) * NT)
                done, rz = O[:, nb % 2], o_rz[nb % 2]
                dve.reciprocal(rz[:, :], done[:, :, HD]).then_inc(o_rz_ready, 1)
                dst = ctxt[:, :].rearrange("p (t w) -> p t w", w=P)[:, nb * TPB:(nb + 1) * TPB, s * HD:(s + 1) * HD]
                ge(dve, o_rz_ready, h * NB + (nb + 1))
                dve.tensor_tensor(dst, done[:, :, 0:HD], each(rz[:, :], HD), ALU.mult).then_inc(ctx_ready, 1)

            def job(x, k):
                kind, n = x.jobs[k]
                nxt = 1 - x.s
                if kind == "W":
                    ge(dve, job_ready, x.job(k) + 1)
                    dve.tensor_tensor(blk(yT, n), blk(yT, n), bank(W_BANK), ALU.add).then_inc(job_done, 1)

            def projection(x, n):
                nxt = 1 - x.s
                ge(dve, proj_done, x.g * NB + (n + 1))
                high = blk(k_stack[nxt], n)
                dve.tensor_copy(high, kq32[n % 2][:, :]).then_inc(rounded, 1)
                ge(dve, rounded, x.g * NB + (n + 1))
                dve.tensor_tensor(blk(q_stack[nxt], n), kq32[n % 2][:, :], high.bitcast(F32), ALU.subtract).then_inc(split, 1)

            def body(x):
                nxt = 1 - x.s
                for k in range(STEPS):
                    if x.prep and k == 0:
                        ge(dve, w_loaded[nxt], x.weights * 32 + 32)
                        dve.tensor_scalar(kq_cols[nxt][:, 0:1], head_cols[nxt][:, 1:2], float(HD) ** -0.5, None,
                                          ALU.mult).then_inc(cols_step, 1)
                        ge(dve, cols_step, x.g * 2 + 1)
                        dve.tensor_tensor(kq_cols[nxt][:, 1:2], head_cols[nxt][:, 0:1], kq_cols[nxt][:, 0:1],
                                          ALU.mult).then_inc(cols_step, 1)
                    if x.prep and k - 1 in PROJ_AT:
                        projection(x, PROJ_AT[k - 1])
                    if k - 1 in x.jobs:
                        job(x, k - 1)
                    if x.prep:
                        for u in max_units(k):
                            ge(dve, max_mm, x.g * MU + (u + 1))
                            at = max_tile(u)[0] * NB + max_tile(u)[1]
                            dve.reduce_max(maxima[:, at:at + 1], bank(M_BANK + u % 2), AX_X).then_inc(max_taken, 1)
                        if k in TOPS_AT:
                            n = TOPS_AT[k]
                            ge(dve, max_taken, x.g * MU + (n + 1) * MU // 2)
                            dve.tensor_reduce(top[:, n * 8:(n + 1) * 8], maxima[:, n * MU // 2:(n + 1) * MU // 2].rearrange(
                                "p (t b) -> p t b", b=NB), AX_X, ALU.max).then_inc(top_ready, 1)
                        if k == (8 if x.main else STEPS - 1):
                            if x.main:
                                ge(dve, pv_done, x.h * STEPS)
                            else:
                                dve.wait_ge(constants_set, V_ONES_SET)
                                dve.wait_ge(v_low, VALUE_UNITS)
                                dve.wait_ge(y_started, 1)
                            head = (x.h + 1).value()
                            dve.tensor_copy(v_head[nxt][:, :].rearrange("p (t w) -> p t w", w=VW),
                                            values[:, :, head, :]).then_inc(v_moved, 1)
                    if x.main and lower_on_vector((k - 1) % NT):
                        lower(dve, x, k - 1, low_vector)
                    if x.main and k % NT == LAG:
                        if k >= NT:
                            contexts(x.h, x.s, k // NT - 1)
                        elif not x.start:
                            contexts(x.h - 1, 1 - x.s, NB - 1)

            dve.tensor_scalar(yT[:, :], xnT[:, :], K.col(C_BO), None, ALU.add).then_inc(y_started, 1)
            dve.wait_ge(constants_set, V_BIAS_SET)
            dve.wait_ge(v_loaded, 32)
            dve.tensor_copy(v_bias[0:1, :], bv).then_inc(v_bias_step, 1)
            dve.wait_ge(v_bias_step, 1)
            dve.tensor_tensor(v_bias_low, bv, v_bias[0:1, :].bitcast(F32), ALU.subtract).then_inc(v_bias_step, 1)
            run(dve, body)
            contexts(Count(0, 0, H - 1), 1, NB - 1)
            for k in TURN[0]:
                job(tail(), k)


def end_of_first_block(nc, K):
    ps, ident = K.ps, K.ident
    with ExitStack() as ctx:
        sb = lambda n, w: ctx.enter_context(nc.sbuf_tensor(n, [P, w], F32))
        sem = lambda n: ctx.enter_context(nc.semaphore(n))
        x, y, s, xn = sb("d_x", N), sb("d_y", N), sb("d_s", N), sb("d_xn", N)
        norm_y, norm_x = Norm(ctx, nc, "d_ny"), Norm(ctx, nc, "d_nx")
        x_loaded, y_turned, y_ready, s_step, s_ready, gated, x1_ready, xn_ready, xn_turned, xn1T_ready = (
            sem(f"d_{n}") for n in ("x_loaded", "y_turned", "y_ready", "s_step", "s_ready", "gated", "x1_ready",
                                    "xn_ready", "xn_turned", "xn1T_ready"))
        block = ctx.enter_context(nc.Block())

        @block.sync
        def _(sp):
            sp.dma_start(x[:, :].rearrange("p (t d) -> p t d", d=D),
                         K.x.rearrange("(t p) d -> p t d", p=P)).then_inc(x_loaded, 16)

        @block.tensor
        def _(pe):
            def turn(src, t, base, done):
                pe.transpose(ps[:, base + t // TPB, (t % TPB) * P:(t % TPB + 1) * P], src[:, t * P:(t + 1) * P],
                             ident[:, :]).then_inc(done, 1)

            for t in range(NT):
                turn(K.yT, t, 0, y_turned)
            for t in range(NT):
                pe.wait_ge(xn_ready, t + 1)
                turn(xn, t, NB, xn_turned)

        @block.scalar
        def _(act):
            for b in range(NB):
                act.wait_ge(y_turned, TPB * (b + 1))
                act.activation(blk(y, b), ps[:, b, :], ACT.Copy).then_inc(y_ready, 1)
            norm_y.scalar(act)
            norm_x.scalar(act)
            for b in range(NB):
                act.wait_ge(xn_turned, TPB * (b + 1))
                act.activation(blk(K.xn1T, b), ps[:, NB + b, :], ACT.Copy).then_inc(xn1T_ready, 1)

        @block.vector
        def _(dve):
            affine_norm(dve, K, norm_y, y, s, y_ready, s_step, s_ready, "gamma", "beta")
            dve.wait_ge(x_loaded, 16)
            for b in range(NB):
                dve.wait_ge(s_ready, b + 1)
                dve.tensor_tensor(blk(s, b), blk(s, b), blk(K.g0, b), ALU.mult).then_inc(gated, 1)
            for b in range(NB):
                dve.wait_ge(gated, b + 1)
                dve.tensor_tensor(blk(K.x1, b), blk(s, b), blk(x, b), ALU.add).then_inc(x1_ready, 1)
            norm_x.vector(dve, K.x1, lambda t: dve.wait_ge(x1_ready, t // TPB + 1))
            for t in range(NT):
                norm_x.apply(dve, xn, K.x1, t, xn_ready)


def widths(mt, nb):
    return max(0, mt - nb * TPB) * P


def second_block(nc, K):
    ps, ident, xT = K.ps, K.ident, K.xn1T
    SCALE = float(D) ** -0.5
    tiles = [(mt, nb) for mt in range(NT) for nb in range(mt // TPB, NB)]
    place = {}
    at = 0
    for tile in tiles:
        place[tile] = at
        at += BLK - widths(*tile)
    SW, NTILES = at, len(tiles)
    with ExitStack() as ctx:
        sb = lambda n, w: ctx.enter_context(nc.sbuf_tensor(n, [P, w], F32))
        sem = lambda n: ctx.enter_context(nc.semaphore(n))
        wq, wk, wv, gw = sb("a1_wq", D), sb("a1_wk", D), sb("a1_wv", D), sb("f1_router_w", E0)
        with ExitStack() as inner:
            qT, kT, v = (inner.enter_context(nc.sbuf_tensor(f"a1_{n}", [P, N], F32)) for n in ("qT", "kT", "v"))
            S = inner.enter_context(nc.sbuf_tensor("a1_scores", [P, SW], F32))
            maxima, sums = (inner.enter_context(nc.sbuf_tensor(f"a1_{n}", [P, NTILES], F32)) for n in ("maxima", "sums"))
            small = inner.enter_context(nc.sbuf_tensor("a1_small", [P, 8], F32))
            ones = inner.enter_context(nc.sbuf_tensor("a1_ones", [P, P], F32))
            loaded, q_mm, q_ready, v_mm, v_ready = (sem(f"a1_{n}") for n in ("loaded", "q_mm", "q_ready", "v_mm", "v_ready"))
            s_mm, s_copied, s_masked, s_maxed, m_step, m_turned, m_spread, m_ready = (
                sem(f"a1_{n}") for n in ("s_mm", "s_copied", "s_masked", "s_maxed", "m_step", "m_turned", "m_spread", "m_ready"))
            e_done, z_ready, z_spread, rz_ready, pv_mm, s_ready, ones_ready = (
                sem(f"a1_{n}") for n in ("e_done", "z_ready", "z_spread", "rz_ready", "pv_mm", "s_ready", "ones_ready"))
            scores = lambda mt, nb: S[:, place[mt, nb]:place[mt, nb] + BLK - widths(mt, nb)]
            diagonal = [t for t in tiles if t[0] // TPB == t[1]]
            block = inner.enter_context(nc.Block())

            @block.sync
            def _(sp):
                for dst, src in ((wq, K.a1_wq), (wk, K.a1_wk), (wv, K.a1_wv), (gw, K.f1_router_w)):
                    sp.dma_start(dst[:, :], src).then_inc(loaded, 16)

            @block.tensor
            def _(pe):
                pe.wait_ge(loaded, 64)
                for n in range(2 * NB):
                    pe.matmul(ps[:, n, :], (wq, wk)[n // NB][:, :], blk(xT, n % NB), start=True, stop=True).then_inc(q_mm, 1)
                for t in range(NT):
                    pe.wait_ge(q_ready, t // TPB + 1)
                    pe.matmul(ps[:, t // TPB, (t % TPB) * P:(t % TPB + 1) * P], xT[:, t * P:(t + 1) * P], wv[:, :],
                              start=True, stop=True).then_inc(v_mm, 1)
                pe.wait_ge(q_ready, 2 * NB)
                for n, (mt, nb) in enumerate(tiles):
                    w = widths(mt, nb)
                    ge(pe, s_copied, n - 3)
                    pe.matmul(ps[:, NB + n % 4, w:BLK], kT[:, mt * P:(mt + 1) * P], qT[:, nb * BLK + w:(nb + 1) * BLK],
                              start=True, stop=True).then_inc(s_mm, 1)
                pe.wait_ge(s_copied, NTILES)
                pe.wait_ge(m_step, 1)
                pe.transpose(ps[0:1, NB, 0:P], small[:, 0:1], ident[:, :]).then_inc(m_turned, 1)
                pe.wait_ge(m_step, 2)
                pe.wait_ge(ones_ready, 1)
                pe.matmul(ps[:, NB + 1, 0:1], ones[0:1, :], small[0:1, 1:2], start=True, stop=True).then_inc(m_spread, 1)
                pe.wait_ge(v_ready, NB)
                for mt in range(NT):
                    for nb in range(mt // TPB, NB):
                        w = widths(mt, nb)
                        pe.wait_ge(e_done, tiles.index((mt, nb)) + 1)
                        mm = pe.matmul(ps[:, nb, w:BLK], v[:, mt * P:(mt + 1) * P], scores(mt, nb), start=(mt == 0),
                                       stop=(mt == nb * TPB + TPB - 1), skip_group_check=True)
                    if mt % TPB == TPB - 1:
                        mm.then_inc(pv_mm, 1)
                pe.wait_ge(z_ready, 1)
                pe.matmul(ps[:, NB + 2, 0:1], ones[:, :], small[:, 4:5], start=True, stop=True).then_inc(z_spread, 1)

            @block.gpsimd
            def _(pool):
                pool.memset(ones[:, :], 1.0).then_inc(ones_ready, 1)
                for mt, nb in diagonal:
                    pool.wait_ge(s_copied, tiles.index((mt, nb)) + 1)
                    s = scores(mt, nb)[:, 0:P]
                    pool.affine_select(out=s, in_=s, compare_op=ALU.is_ge, fill=-BIG, base=0, pattern=[[1, P]],
                                       channel_multiplier=-1).then_inc(s_masked, 1)

            @block.scalar
            def _(act):
                act.wait_ge(q_mm, 1)
                for n in range(2 * NB):
                    act.wait_ge(q_mm, n + 1)
                    act.activation(blk((qT, kT)[n // NB], n % NB), ps[:, n, :], ACT.Identity,
                                   bias=K.col((C_Q1B, C_K1B)[n // NB])).then_inc(q_ready, 1)
                for n, (mt, nb) in enumerate(tiles):
                    act.wait_ge(s_mm, n + 1)
                    act.activation(scores(mt, nb), ps[:, NB + n % 4, widths(mt, nb):BLK], ACT.Copy).then_inc(s_copied, 1)
                act.wait_ge(m_spread, 1)
                act.activation(small[:, 2:3], ps[:, NB + 1, 0:1], ACT.Copy, scale=-SCALE).then_inc(m_ready, 1)
                act.wait_ge(m_ready, 1)
                act.wait_ge(s_masked, len(diagonal))
                act.wait_ge(s_maxed, NTILES)
                for n, (mt, nb) in enumerate(tiles):
                    act.activation(scores(mt, nb), scores(mt, nb), ACT.Exp, bias=small[:, 2:3], scale=SCALE,
                                   accum_out=sums[:, n:n + 1]).then_inc(e_done, 1)

            @block.vector
            def _(dve):
                for b in range(NB):
                    dve.wait_ge(v_mm, TPB * (b + 1))
                    dve.tensor_tensor(blk(v, b).rearrange("p (t d) -> p t d", d=D),
                                      ps[:, b, :].rearrange("p (t d) -> p t d", d=D),
                                      spread(K.row("v1b"), TPB), ALU.add).then_inc(v_ready, 1)
                for n, (mt, nb) in enumerate(tiles):
                    if (mt, nb) in diagonal:
                        dve.wait_ge(s_masked, diagonal.index((mt, nb)) + 1)
                    dve.wait_ge(s_copied, n + 1)
                    dve.reduce_max(maxima[:, n:n + 1], scores(mt, nb), AX_X).then_inc(s_maxed, 1)
                dve.wait_ge(s_maxed, NTILES)
                dve.reduce_max(small[:, 0:1], maxima[:, :], AX_X).then_inc(m_step, 1)
                dve.wait_ge(m_turned, 1)
                dve.reduce_max(small[0:1, 1:2], ps[0:1, NB, 0:P], AX_X).then_inc(m_step, 1)
                dve.wait_ge(e_done, NTILES)
                dve.reduce_sum(small[:, 4:5], sums[:, :], AX_X).then_inc(z_ready, 1)
                dve.wait_ge(z_spread, 1)
                dve.reciprocal(small[:, 5:6], ps[:, NB + 2, 0:1]).then_inc(rz_ready, 1)
                dve.wait_ge(rz_ready, 1)
                for b in range(NB):
                    dve.wait_ge(pv_mm, b + 1)
                    dve.tensor_scalar(blk(K.sT, b), ps[:, b, :], small[:, 5:6], None, ALU.mult).then_inc(s_ready, 1)

        w1 = [sb(f"f1_w1_{h}", FT1 * P) for h in range(2)]
        w3 = [sb(f"f1_w3_{h}", FT1 * P) for h in range(2)]
        w2 = [sb(f"f1_w2_{h}", FT1 * D) for h in range(2)]
        cb = [sb(f"f1_weight_{h}", N) for h in range(2)]
        SLOTS = 8
        hg, hu, hs = sb("f1_gate", SLOTS * BLK), sb("f1_product", SLOTS * BLK), sb("f1_hidden", SLOTS * BLK)
        cT = ctx.enter_context(nc.sbuf_tensor("f1_combineT", [E0, N], F32))
        one_row = ctx.enter_context(nc.sbuf_tensor("f1_one", [1, N], F32))
        g1 = sb("f1_g", N)
        o = sb("f1_out", N)
        router = Router(ctx, nc, "f1")
        w_loaded = [sem(f"f1_w_loaded{h}") for h in range(2)]
        logits_mm, c_turned, cT_ready, one_ready, c_stored = (
            sem(f"f1_{n}") for n in ("logits_mm", "c_turned", "cT_ready", "one_ready", "c_stored"))
        h_mm, h_gated, h_mult, h_ready, y_mm, g_ready, p_ready, p_turned, o_ready, o_stored = (
            sem(f"f1_{n}") for n in ("h_mm", "h_gated", "h_mult", "h_ready", "y_mm", "g_ready", "p_ready",
                                     "p_turned", "o_ready", "o_stored"))
        UE = NB * FT1
        block = ctx.enter_context(nc.Block())

        @block.sync
        def _(sp):
            def weights(e, s):
                sp.dma_start(w1[s][:, :], K.f1_w1[e]).then_inc(w_loaded[s], 16)
                sp.dma_start(w3[s][:, :], K.f1_w3[e]).then_inc(w_loaded[s], 16)
                sp.dma_start(w2[s][:, :].rearrange("p (k d) -> p k d", d=D),
                             K.f1_w2[e].rearrange("(k p) d -> p k d", p=P)).then_inc(w_loaded[s], 16)

            def weighting(e, s):
                sp.dma_start(cb[s][:, :], K.combine1_dram[e].broadcast_to([P, N])).then_inc(w_loaded[s], 16)

            weights(0, 1)
            weights(1, 0)
            sp.wait_ge(one_ready, 1)
            sp.dma_start(K.combine1_dram[0], one_row[:, :]).then_inc(c_stored, 16)
            sp.wait_ge(c_stored, 16)
            weighting(0, 1)
            sp.wait_ge(cT_ready, NB)
            sp.dma_start(K.combine1_dram.rearrange("e o n -> (e o) n")[1:E1, :], cT[:, :]).then_inc(c_stored, 16)
            sp.wait_ge(c_stored, 32)
            weighting(1, 0)
            sp.wait_ge(y_mm, UE)
            weights(2, 1)
            weighting(2, 1)
            with sp.Fori(1, E0 // 2) as i:
                for s in range(2):
                    sp.wait_ge(y_mm, i * (2 * UE) + s * UE)
                    weights(i * 2 + (1 + s), s)
                    weighting(i * 2 + (1 + s), s)
            sp.wait_ge(o_ready, NB)
            sp.dma_start(K.out.rearrange("(t p) d -> p t d", p=P), o[:, :].rearrange("p (t d) -> p t d", d=D)).then_inc(o_stored, 16)
            sp.wait_ge(o_stored, 16)

        def experts(eng, body):
            body(1, 0, 0)
            for s in range(2):
                body(s, 0, UE * (1 + s))
            with eng.Fori(1, E0 // 2) as i:
                for s in range(2):
                    body(s, i, i * (2 * UE) + UE * (1 + s))

        @block.tensor
        def _(pe):
            for t in range(NT):
                mm = pe.matmul(ps[:, 0, t * E0:(t + 1) * E0], xT[:, t * P:(t + 1) * P], gw[:, :], start=True, stop=True)
            mm.then_inc(logits_mm, 1)
            pe.wait_ge(router.sem, Router.STEPS)
            for t in range(NT):
                pe.transpose(ps[0:E0, t // TPB, (t % TPB) * P:(t % TPB + 1) * P], router.w[:, t * E0:(t + 1) * E0],
                             ident[:, :]).then_inc(c_turned, 1)
            pe.wait_ge(cT_ready, NB)

            def out_product(u, s, b, ft, start=False):
                pe.wait_ge(h_ready, u + 1)
                pe.matmul(ps[:, NB + b, :], w2[s][:, ft * D:(ft + 1) * D], blk(hs, b * FT1 + ft), start=start, stop=True,
                          skip_group_check=True).then_inc(y_mm, 1)

            def body(s, i, u0):
                shared = isinstance(u0, int) and u0 == 0
                second = isinstance(u0, int) and u0 == UE
                pe.wait_ge(w_loaded[s], 64 if shared else (i * 64 + (128 if s else 64)))
                for b in range(NB):
                    for ft in range(FT1):
                        ge(pe, h_mult, u0 + (b * FT1 + ft - 1))
                        pe.matmul(ps[:, ft, :], w1[s][:, ft * P:(ft + 1) * P], blk(xT, b), start=True, stop=True)
                        pe.matmul(ps[:, FT1 + ft, :], w3[s][:, ft * P:(ft + 1) * P], blk(xT, b), start=True,
                                  stop=True).then_inc(h_mm, 1)
                    if not (shared and b == 0):
                        for ft in range(FT1):
                            out_product(u0 + ((b - 1) * FT1 + ft), s if b else 1 - s, (b - 1) % NB, ft,
                                        start=(ft == 0 and (shared or (second and b == 0))))

            experts(pe, body)
            for ft in range(FT1):
                out_product(E1 * UE - FT1 + ft, 1, NB - 1, ft)
            for t in range(NT):
                pe.wait_ge(p_ready, t // TPB + 1)
                pe.transpose(ps[:, t // TPB, (t % TPB) * P:(t % TPB + 1) * P], o[:, t * P:(t + 1) * P],
                             ident[:, :]).then_inc(p_turned, 1)

        @block.scalar
        def _(act):
            router.scalar(act, Router.LOGITS)
            for b in range(NB):
                act.wait_ge(c_turned, TPB * (b + 1))
                act.activation(blk(cT, b), ps[0:E0, b, :], ACT.Copy).then_inc(cT_ready, 1)

            def body(s, i, u0):
                for b in range(NB):
                    for ft in range(FT1):
                        k = b * FT1 + ft
                        act.wait_ge(h_mm, u0 + (k + 1))
                        ge(act, h_mult, u0 + (k - SLOTS + 1))
                        act.activation(blk(hg, k), ps[:, ft, :], ACT.Silu).then_inc(h_gated, 1)

            experts(act, body)
            for b in range(NB):
                act.wait_ge(y_mm, E1 * UE - (NB - 1 - b) * FT1)
                act.activation(blk(g1, b), ps[:, NB + b, :], ACT.Silu).then_inc(g_ready, 1)

        @block.vector
        def _(dve):
            dve.memset(one_row[:, :], 1.0).then_inc(one_ready, 1)
            dve.wait_ge(logits_mm, 1)
            router.vector(dve, ps[:, 0, 0:NT * E0], None)

            def body(s, i, u0):
                for b in range(NB):
                    for ft in range(FT1):
                        k = b * FT1 + ft
                        dve.wait_ge(h_gated, u0 + (k + 1))
                        ge(dve, h_ready, u0 + (k - SLOTS + 1))
                        dve.tensor_tensor(blk(hu, k), blk(hg, k), ps[:, FT1 + ft, :], ALU.mult).then_inc(h_mult, 1)

            experts(dve, body)
            for b in range(NB):
                dve.wait_ge(g_ready, b + 1)
                dve.tensor_tensor(blk(o, b), blk(K.sT, b), blk(g1, b), ALU.mult).then_inc(p_ready, 1)
            for b in range(NB):
                dve.wait_ge(p_turned, TPB * (b + 1))
                dve.tensor_tensor(blk(o, b), ps[:, b, :], blk(K.x1, b), ALU.add).then_inc(o_ready, 1)

        @block.gpsimd
        def _(pool):
            def body(s, i, u0):
                shared = isinstance(u0, int) and u0 == 0
                pool.wait_ge(w_loaded[s], 64 if shared else (i * 64 + (128 if s else 64)))
                for b in range(NB):
                    for ft in range(FT1):
                        k = b * FT1 + ft
                        pool.wait_ge(h_mult, u0 + (k + 1))
                        ge(pool, y_mm, u0 + (k - SLOTS + 1))
                        pool.tensor_tensor(blk(hs, k), blk(hu, k), blk(cb[s], b), ALU.mult).then_inc(h_ready, 1)

            experts(pool, body)


def two_blocks_kernel(nc, t, out, stop_after=99):
    with ExitStack() as ctx:
        K = Kit()
        K.out = out
        (K.x, K.cols_dram, K.rows_dram, K.f0_wv, K.f0_wo, K.f0_gate_w, K.f0_b2, K.f0_w1, K.f0_w2, K.f0_b1,
         K.a0_wv, K.a0_bv, K.a0_wkq, K.a0_cols, K.a0_wo, K.a1_wq, K.a1_wk, K.a1_wv, K.f1_router_w, K.f1_w1,
         K.f1_w3, K.f1_w2) = (t[n] for n in NAMES)
        K.combine_dram = nc.dram_tensor("combine0", [E0, 1, N], F32, kind="Internal").ap()
        K.combine1_dram = nc.dram_tensor("combine1", [E1, 1, N], F32, kind="Internal").ap()
        sb = lambda n, w, dt=F32: ctx.enter_context(nc.sbuf_tensor(n, [P, w], dt))
        K.ps = ctx.enter_context(nc.psum_tensor("ps", [P, 8, BLK], F32))
        K.ident, K.cols, K.rows = sb("ident", P), sb("cols", NCOL), sb("rows", NROW)
        K.g0 = sb("g0", N)
        K.ident_ready = ctx.enter_context(nc.semaphore("ident_ready"))
        K.consts_loaded = ctx.enter_context(nc.semaphore("consts_loaded"))
        with ExitStack() as first:
            K.yT = first.enter_context(nc.sbuf_tensor("yT", [P, N], F32))
            with ExitStack() as a:
                K.xnT = a.enter_context(nc.sbuf_tensor("xnT", [P, N], F32))
                load_and_normalise(nc, K)
                gate_of_first_block(nc, K)
                K.values = a.enter_context(nc.sbuf_tensor("values", [P, NT * H * VW], F16))
                attention_of_first_block(nc, K)
            K.x1, K.xn1T = (first.enter_context(nc.sbuf_tensor(n, [P, N], F32)) for n in ("x1", "xn1T"))
            K.sT = K.yT
            end_of_first_block(nc, K)
            second_block(nc, K)


NAMES = ("x", "cols", "rows", "f0_wv", "f0_wo", "f0_gate_w", "f0_b2", "f0_w1", "f0_w2", "f0_b1", "a0_wv", "a0_bv",
         "a0_wkq", "a0_cols", "a0_wo", "a1_wq", "a1_wk", "a1_wv", "f1_router_w", "f1_w1", "f1_w3", "f1_w2")


def layout(i):
    import numpy as np
    i = {k: np.asarray(v) for k, v in i.items()}
    heads = lambda w: w.reshape(H, HD, D).transpose(0, 2, 1)
    root = np.full((H, HD), float(HD) ** 0.5, np.float32)
    head_cols = np.stack([np.concatenate([i["L0_attn_bk"].reshape(H, HD), i["L0_attn_bq"].reshape(H, HD)], axis=1),
                          np.concatenate([root, np.repeat(i["L0_attn_adaptive_scale"][:, None], HD, axis=1)], axis=1)],
                         axis=2)
    cols = np.concatenate([np.stack([i["L0_attn_bo"], i["L0_ffn_in_proj_b"][2 * D:], i["L0_ffn_out_b"],
                                     i["L1_attn_bq"], i["L1_attn_bk"]]), i["L0_ffn_b1"].reshape(E0 * FT0, P)]).T
    rows = np.concatenate([i[n] for n in ("L0_ffn_ln1_g", "L0_ffn_ln1_b", "L0_ffn_ln2_g", "L0_ffn_ln2_b",
                                          "L0_attn_gamma", "L0_attn_beta", "L1_attn_bv", "L0_ffn_gate_b")])
    t = {
        "x": i["L0_attn_x"].reshape(N, D), "cols": cols, "rows": rows[None],
        "f0_wv": i["L0_ffn_in_proj_w"][2 * D:].T, "f0_wo": i["L0_ffn_out_w"].T, "f0_gate_w": i["L0_ffn_gate_w"].T,
        "f0_b2": i["L0_ffn_b2"], "f0_w1": i["L0_ffn_w1"].transpose(0, 2, 1),
        "f0_w2": i["L0_ffn_w2"].transpose(0, 2, 1).reshape(E0, FT0, P, D).transpose(0, 2, 1, 3).reshape(E0, P, FT0 * D),
        "f0_b1": i["L0_ffn_b1"].reshape(E0, FT0, P).transpose(0, 2, 1),
        "a0_wv": i["L0_attn_Wv"].T, "a0_bv": i["L0_attn_bv"][None],
        "a0_wkq": np.concatenate([heads(i["L0_attn_Wk"]), heads(i["L0_attn_Wq"])], axis=2),
        "a0_cols": head_cols, "a0_wo": i["L0_attn_Wo"].T.reshape(H // 2, P, D),
        "a1_wq": i["L1_attn_Wq"], "a1_wk": i["L1_attn_Wk"], "a1_wv": i["L1_attn_Wv"], "f1_router_w": i["L1_ffn_w_router"],
        "f1_w1": np.concatenate([i["L1_ffn_sw1"][None], i["L1_ffn_w1"]]),
        "f1_w3": np.concatenate([i["L1_ffn_sw3"][None], i["L1_ffn_w3"]]),
        "f1_w2": np.concatenate([i["L1_ffn_sw2"][None], i["L1_ffn_w2"]]),
    }
    return {n: np.ascontiguousarray(a) for n, a in t.items()}


def kernel(**inputs):
    import concourse.bacc as _bacc
    from concourse.bass_utils import run_bass_kernel_spmd as _run

    nc = _bacc.Bacc("TRN2", target_bir_lowering=False, num_devices=1)
    arrays = {f"in_{n}": a for n, a in layout(inputs).items()}
    aps = {n: nc.dram_tensor(f"in_{n}", arrays[f"in_{n}"].shape, F32, kind="ExternalInput").ap() for n in NAMES}
    out = nc.dram_tensor("out", (N, D), F32, kind="ExternalOutput").ap()
    two_blocks_kernel(nc, aps, out)
    r = _run(nc, [arrays], core_ids=[0])
    return r.results[0]["out"].reshape(1, N, D)
```
